# Optimizing a Trainium2 kernel written in Bass

```python
import numpy as np
import jax
import jax.numpy as jnp

def _softmax(x, axis=-1):
    return jax.nn.softmax(x, axis=axis)

def _gelu(x):
    return jax.nn.gelu(x, approximate=True)

def _silu(x):
    return jax.nn.silu(x)

def _sigmoid(x):
    return jax.nn.sigmoid(x)

def _layernorm(x, axis=-1, eps=1e-05):
    m = jnp.mean(x, axis=axis, keepdims=True)
    v = jnp.var(x, axis=axis, keepdims=True)
    return (x - m) / jnp.sqrt(v + eps)

def _scatter_add(tgt, idx, src, axis=0):
    return tgt.at[idx].add(src)

def _segment_sum(src, seg, n):
    return jax.ops.segment_sum(src, seg, n)
kernel_name = 'mk_flamingo_gated_d1_seqx_r4_92b591'

def setup_inputs(seed: int=0):
    np.random.seed(seed)
    _w = jnp.asarray

    def _rec_inputs():
        import jax
        import jax.numpy as jnp
        _rk = jax.random.key(seed)
        x = -7.109e-05 + 0.9999 * jax.random.normal(jax.random.fold_in(_rk, 1), (8, 100, 1024), jnp.float32)
        _lenS = 100 - jax.random.randint(jax.random.fold_in(_rk, 7), (8,), 0, max(1, 100 // 4) + 1, jnp.int32)
        _lenS2 = 361 - jax.random.randint(jax.random.fold_in(_rk, 8), (8,), 0, max(1, 361 // 4) + 1, jnp.int32)
        _ctx_4096P = jax.random.normal(jax.random.fold_in(_rk, 11), (8, 16, 1024), jnp.float32)
        _ctx_4096c = jax.random.dirichlet(jax.random.fold_in(_rk, 511), 0.3 * jnp.ones((16,), jnp.float32), (8, 361))
        _ctx_4096t = jnp.einsum('bsk,bkd->bsd', _ctx_4096c, _ctx_4096P)
        _ctx_4096t = _ctx_4096t * jax.lax.rsqrt(jnp.mean(jnp.square(_ctx_4096t)) + 1e-12) * 0.953939
        ctx_4096 = -0.00010331 + 0.999899 * (_ctx_4096t + 0.3 * jax.random.normal(jax.random.fold_in(_rk, 611), (8, 361, 1024), jnp.float32))
        _g = jax.random.normal(jax.random.fold_in(_rk, 9001), (2, 1), jnp.float32)
        _g = jnp.sign(_g) * jnp.maximum(jnp.abs(_g), 1.0) + (_g == 0) * 1.0
        g_xattn = _g[0]
        g_ffn = _g[1]
        return (x, ctx_4096, g_xattn, g_ffn)
    x, ctx_4096, g_xattn, g_ffn = _rec_inputs()

    def _L0_xattn_setup():
        import jax, jax.numpy as jnp
        import numpy as np
        key = jax.random.key(seed)
        k1, k2 = jax.random.split(key)
        B, Lq, Lk, D = (16, 256, 512, 1024)
        query = jax.random.normal(k1, (B, Lq, D), dtype=jnp.float32)
        key_t = jax.random.normal(k2, (B, Lk, D), dtype=jnp.float32)
        return {'query': query, 'key': key_t}
    _L0_xattn_all = _L0_xattn_setup()
    _L0_xattn_in = {k: v for k, v in _L0_xattn_all.items() if k in ()}
    del _L0_xattn_all

    def _L0_ffn_setup():
        import jax, jax.numpy as jnp
        import numpy as np
        TOP_K = 2
        key = jax.random.key(seed)
        k0, k1, k2 = jax.random.split(key, 3)
        B, S, D, H, E = (4, 512, 1024, 1024, 8)
        sc = 1.0 / np.sqrt(D).astype(np.float32)
        x = jax.random.normal(k0, (B, S, D), dtype=jnp.float32)
        W_gate = jax.random.normal(k1, (D, E), dtype=jnp.float32) * sc
        b_gate = jnp.zeros((E,), dtype=jnp.float32)
        W_e = jax.random.normal(k2, (E, D, H), dtype=jnp.float32) * sc
        b_e = jnp.zeros((E, H), dtype=jnp.float32)
        return {'x': x, 'W_gate': W_gate, 'b_gate': b_gate, 'W_e': W_e, 'b_e': b_e}
    _L0_ffn_all = _L0_ffn_setup()
    _L0_ffn_in = {k: v for k, v in _L0_ffn_all.items() if k in ('W_gate', 'b_gate', 'W_e', 'b_e')}
    del _L0_ffn_all
    return {'x': x, 'ctx_4096': ctx_4096, 'g_xattn': g_xattn, 'g_ffn': g_ffn, 'L0_ffn_W_gate': _L0_ffn_in['W_gate'], 'L0_ffn_b_gate': _L0_ffn_in['b_gate'], 'L0_ffn_W_e': _L0_ffn_in['W_e'], 'L0_ffn_b_e': _L0_ffn_in['b_e']}

def reference(x, ctx_4096, g_xattn, g_ffn, L0_ffn_W_gate, L0_ffn_b_gate, L0_ffn_W_e, L0_ffn_b_e):
    import jax
    import jax.numpy as jnp

    def _L0_xattn_ref(query, key):
        import jax, jax.numpy as jnp
        import numpy as np
        a = jnp.einsum('bqd,bkd->bqk', query, key)
        e = jax.nn.softmax(a, axis=-1)
        c = jnp.einsum('bqk,bkd->bqd', e, key)
        return c

    def _L0_ffn_ref(x, W_gate, b_gate, W_e, b_e):
        import jax, jax.numpy as jnp
        import numpy as np
        TOP_K = 2
        logits = x @ W_gate + b_gate
        _, top_idx = jax.lax.top_k(logits, TOP_K)
        y_all = jax.nn.relu(jnp.einsum('bsd,edh->bseh', x, W_e) + b_e)
        y = jnp.take_along_axis(y_all, top_idx[..., None], axis=2)
        return y.mean(axis=2)
    x = x + jnp.tanh(g_xattn[0]) * _L0_xattn_ref(_layernorm(x, axis=-1), ctx_4096)
    x = x + jnp.tanh(g_ffn[0]) * _L0_ffn_ref(_layernorm(x, axis=-1), L0_ffn_W_gate, L0_ffn_b_gate, L0_ffn_W_e, L0_ffn_b_e)
    return x

_drawn_inputs = setup_inputs


def setup_inputs(seed=0):
    import zlib

    import numpy as np

    out = dict(_drawn_inputs(seed))
    spreads = {'L0_ffn_b_gate': (0.0, 0.1), 'L0_ffn_b_e': (0.0, 0.1)}
    factors = {}
    for name, (base, spread) in spreads.items():
        noise = np.random.default_rng([zlib.crc32(name.encode()), seed]).standard_normal(out[name].shape)
        drawn = base * np.exp(spread * noise) if base else spread * noise
        out[name] = jnp.asarray(drawn.astype(out[name].dtype))
    for name, factor in factors.items():
        out[name] = (out[name] * factor).astype(out[name].dtype)
    return out
```

```python
from contextlib import ExitStack

import concourse.bass as bass
from concourse import mybir

F32 = mybir.dt.float32
F32R = mybir.dt.float32r
F16 = mybir.dt.float16
I32 = mybir.dt.int32
ALU = mybir.AluOpType
ACT = mybir.ActivationFunctionType
AX = mybir.AxisListType

P = 128
EPS = 1e-5
TOP_K = 2
STATIC_TILES = 2
FAR = 1000


def gated_block(nc, x, ctx_kv, g_xattn, g_ffn, w_gate, b_gate, w_e, b_e, out):
    B, Q, D = x.shape
    KV = ctx_kv.shape[1]
    E = w_gate.shape[1]
    H = w_e.shape[2]
    KD = D // P
    HB = H // 2
    N_TOK = B * Q
    KV_T = [(a, min(P, KV - a)) for a in range(0, KV, P)]
    LAST = len(KV_T) - 1
    MAX_TILES = -(-N_TOK // P)
    OVER = MAX_TILES - STATIC_TILES
    COLS = E * MAX_TILES
    assert out.shape[0] == N_TOK + P and H == D and E == KD and B % 2 == 0 and E % 2 == 0
    assert N_TOK < FAR

    es = ExitStack()
    with es:
        def sb(name, shape, dt=F32, stack=es):
            return stack.enter_context(nc.sbuf_tensor(name, shape, dt))

        def sem(name):
            return es.enter_context(nc.semaphore(name))

        hn_rows = nc.dram_tensor("hn_rows", [N_TOK + P, D], F32, kind="Internal").ap()

        ident = sb("ident", [P, P])
        before = sb("before", [Q, Q], F16)
        ones = sb("ones", [Q, Q], F16)
        iota_slot = sb("iota_slot", [Q, P])
        iota_col = sb("iota_col", [Q, COLS])
        expert_base = sb("expert_base", [Q, E])
        choice_no = sb("choice_no", [Q, TOP_K, E])
        tok_far = sb("tok_far", [Q, B])
        spare_row = sb("spare_row", [P, 1])
        used_shift = sb("used_shift", [P, 1])
        seed_bits = sb("seed_bits", [Q, 2], I32)
        lower_e = sb("lower_e", [Q, E, E])
        wg = sb("wg", [P, KD, E])
        bg = sb("bg", [P, E])
        gx = sb("gx", [P, 1])
        gf = sb("gf", [P, 1])
        tgx = sb("tgx", [P, 1])
        tgf = sb("tgf", [P, 1])
        tgf_half = sb("tgf_half", [P, 1])
        tile_table = sb("tile_table", [1, 2, E], I32)
        slot_token = sb("slot_token", [P, COLS], I32)
        idx_now = sb("idx_now", [P, 2 * STATIC_TILES + 1], I32)

        raw = sb("raw", [P, KD, H])
        wh = [sb("wh0", [P, KD, H], F32R), None]
        wl = [sb("wl0", [P, KD, H], F32R), None]

        att = ExitStack()
        ctx_t = [sb(f"ctx{p}", [P, len(KV_T), D], stack=att) for p in range(2)]
        ctx_h = sb("ctx_h", [P, len(KV_T), D], F32R, stack=att)
        ctx_l = sb("ctx_l", [P, len(KV_T), D], F32R, stack=att)
        kT = sb("kT", [P, KD, KV], stack=att)
        x_all = sb("x_all", [Q, B, D], stack=att)
        normed = sb("normed", [Q, D], stack=att)
        qT = sb("qT", [P, KD, Q], stack=att)
        probs = sb("probs", [Q, KV], stack=att)
        probsT_h = sb("probsT_h", [P, len(KV_T), Q], F32R, stack=att)
        probsT_l = sb("probsT_l", [P, len(KV_T), Q], F32R, stack=att)
        hnT = sb("hnT", [P, KD, Q], stack=att)
        stats = sb("stats", [Q, 2, 2, 6], stack=att)
        mean_var = sb("mean_var", [Q, 2, 2], stack=att)
        var_eps = sb("var_eps", [Q, 2], stack=att)
        neg_half = sb("neg_half", [Q, 2], stack=att)
        half_bits = sb("half_bits", [Q, 2], I32, stack=att)
        guess = [sb(f"guess{j}", [Q, 2], stack=att) for j in range(NEWTON)]
        guess_sq = sb("guess_sq", [Q, 2], stack=att)
        inv_std = [sb(f"inv_std{p}", [Q, 2], stack=att) for p in range(2)]
        shift = [sb(f"shift{p}", [Q, 2], stack=att) for p in range(2)]
        neg_max = sb("neg_max", [Q, 1], stack=att)
        prob_sum = sb("prob_sum", [Q, 1], stack=att)
        inv_sum = sb("inv_sum", [Q, 1], stack=att)
        coef = sb("coef", [Q, 1], stack=att)
        logit = sb("logit", [Q, E], stack=att)
        above = sb("above", [Q, E, E], stack=att)
        tied = sb("tied", [Q, E, E], stack=att)
        place = sb("place", [Q, E], stack=att)
        onehot = sb("onehot", [Q, TOP_K, E], stack=att)
        chosen = sb("chosen", [Q, E], F16, stack=att)
        chosen_sum = sb("chosen_sum", [Q, E], F16, stack=att)
        slot_of = sb("slot_of", [Q, E], stack=att)
        picked = sb("picked", [Q, TOP_K, E], stack=att)
        slot_i = sb("slot_i", [Q, TOP_K], I32, stack=att)
        slot_col_i = sb("slot_col_i", [Q, TOP_K], I32, stack=att)
        slot_row_i = sb("slot_row_i", [Q, TOP_K], I32, stack=att)
        slot_col = sb("slot_col", [Q, TOP_K], stack=att)
        slot_row = sb("slot_row", [Q, TOP_K], stack=att)
        at_row = sb("at_row", [Q, TOP_K, P], F16, stack=att)
        tok_col = sb("tok_col", [Q, TOP_K, COLS], F16, stack=att)
        slot_acc = sb("slot_acc", [P, COLS], stack=att)
        used = sb("used", [P, COLS], stack=att)
        over_f = sb("over_f", [1, E], stack=att)
        over_i = sb("over_i", [1, E], I32, stack=att)
        over_e = sb("over_e", [1, E], stack=att)
        over_m = sb("over_m", [1, E, E], stack=att)
        over_b = sb("over_b", [1, E], stack=att)
        att.close()

        wh[1] = sb("wh1", [P, KD, H], F32R)
        wl[1] = sb("wl1", [P, KD, H], F32R)
        xg = [sb(f"xg{t}", [P, D]) for t in range(2)]
        xh = [sb(f"xh{t}", [P, KD, P], F32R) for t in range(2)]
        xl = [sb(f"xl{t}", [P, KD, P], F32R) for t in range(2)]
        y = [sb(f"y{t}", [P, H]) for t in range(2)]
        y_over = sb("y_over", [P, H])
        bias = sb("bias", [P, H])

        ps = [es.enter_context(nc.psum_tensor(f"ps{j}", [P, 2 * 512], F32)) for j in range(4)]
        turn_bank = [ps[j // 2][:, 512 * (j % 2):512 * (j % 2) + 512] for j in range(4)]
        score_ps = ps[2][0:Q, 0:KV]
        probsT_ps = ps[2][:, 512:512 + len(KV_T) * Q]
        logit_ps = ps[2][0:Q, 840:840 + E]
        rank_ps = ps[2][0:Q, 860:860 + E]
        slot_ps = ps[2][:, 880:880 + COLS]
        count_ps = ps[2][0:Q, 940:940 + E]
        att_ps = ps[3][0:Q, 0:D]
        xT_ps, over_ps, *y_ps = ps

        s_params = sem("params_loaded")
        s_const0 = sem("const_filled")
        s_const = sem("const_ready")
        s_tanh = sem("tanh_ready")
        s_tgf = sem("tgf_half_ready")
        s_zero = sem("spare_rows_zeroed")
        s_x01 = [sem("x0_loaded"), sem("x1_loaded")]
        s_x = sem("x_rest_loaded")
        s_ctx = [sem(f"ctx_loaded{p}") for p in range(2)]
        s_raw0 = sem("raw_loaded_first")
        s_raw = [sem(f"raw_loaded{k}") for k in range(KD)]
        s_turned = sem("turned")
        s_evac = [sem("evac_act"), sem("evac_dve")]
        s_norm = sem("norm_step")
        s_ln = sem("norm_ready")
        s_qn = sem("qn_ready")
        s_scores = sem("scores_ready")
        s_negmax = sem("neg_max_ready")
        s_probs = sem("probs_ready")
        s_inv = sem("inv_sum_ready")
        s_coef = sem("coef_ready")
        s_pT = sem("probs_turned")
        s_pTh = sem("probsT_high_ready")
        s_pTl = sem("probsT_low_ready")
        s_ch = sem("ctx_high_ready")
        s_cl = sem("ctx_low_ready")
        s_att = sem("attention_ready")
        s_h = sem("h_ready")
        s_hn = sem("hn_ready")
        s_logit_ps = sem("logits_multiplied")
        s_hstore = sem("h_stored")
        s_hnstore = sem("hn_stored")
        s_wh = sem("w_high_ready")
        s_wl = sem("w_low_ready")
        s_wl0 = sem("w_low_ready_first")
        s_wfree = sem("w_used")
        s_choose = sem("choose_step")
        s_chosen = sem("chosen_ready")
        s_chosen_own = sem("onehot_ready")
        s_rank = sem("ranks_ready")
        s_sum = sem("chosen_summed")
        s_slot = sem("slot_step")
        s_tok_col = sem("tok_col_ready")
        s_slots_ps = sem("slots_ready")
        s_acc = sem("slots_added")
        s_count = sem("counts_ready")
        s_last = sem("table_step")
        s_table = sem("tile_table_ready")
        s_slot_token = sem("slot_token_ready")
        s_bias = sem("bias_loaded")
        s_idx = sem("idx_staged")
        s_gath = [sem(f"gathered{t}") for t in range(2)]
        s_xT = [sem(f"x_turned{t}") for t in range(2)]
        s_xh = [sem(f"x_high_ready{t}") for t in range(2)]
        s_xl = [sem(f"x_low_ready{t}") for t in range(2)]
        s_mm0 = sem("tile0_multiplied")
        s_yev = [sem(f"y_evacuated{t}") for t in range(2)]
        s_y = sem("y_ready")
        s_added = sem("y_added")
        o_idx = sem("over_idx_staged")
        o_gath = sem("over_gathered")
        o_xT = sem("over_x_turned")
        o_xh = sem("over_x_high_ready")
        o_xl = sem("over_x_low_ready")
        o_mm = sem("over_multiplied")
        o_yev = sem("over_y_evacuated")
        o_y = sem("over_y_ready")
        o_added = sem("over_y_added")
        o_free = sem("over_y_free")

        def wait_apart(eng, semaphore, value):
            if not isinstance(value, int):
                value = eng.to_reg(value)
            eng.wait_ge(s_const, 1)
            eng.wait_ge(semaphore, value)

        def of_batch(tile, b):
            return tile[:, bass.ds(b, 1), :].rearrange("q a n -> q (a n)")

        def at_k(tile, k):
            return tile[:, bass.ds(k, 1), :].rearrange("p a n -> p (a n)")

        def after(eng, semaphore, value):
            if not (isinstance(value, int) and value == 0):
                eng.wait_ge(semaphore, value)

        def stage1(eng, step):
            step(0, 0)
            step(1, 1)
            with eng.Fori(1, B // 2 - 1) as i:
                step(2 * i, 0)
                step(2 * i + 1, 1)
            for s in range(B - 2, B + 2):
                step(s, s % 2)

        def parts(s):
            if not isinstance(s, int):
                return True, True, True, True, True
            return s < B, 1 <= s <= B, s >= 2, s < B - 1, s < B - 2

        def stage3(eng, expert):
            expert(0, 0, False)
            expert(1, 1, False)
            with eng.Fori(1, E // 2 - 1) as i:
                expert(2 * i, 0, False)
                expert(2 * i + 1, 1, False)
            expert(E - 2, 0, False)
            expert(E - 1, 1, True)

        NEW = KD + 2
        GROUPS = NEW + 2

        def group(s, g):
            if not isinstance(s, int):
                return GROUPS * s - 4 + g
            before_s = sum(NEW * (c < B) + 2 * (c >= 2) for c in range(s))
            return before_s + (g if s < B else g - NEW)

        def group_bank(s, g):
            return turn_bank[(group(s, g) if isinstance(s, int) else g) % 4]

        def evacuated(s, g):
            if not isinstance(s, int):
                return GROUPS // 2 * s - 2 + g // 2 + 1
            return group(s, g) // 2 + 1

        block = es.enter_context(nc.Block())

        @block.sync
        def _(sp):
            def load_parameters():
                sp.dma_start(wg[:, :, :], w_gate.rearrange("(k p) e -> p k e", p=P)).then_inc(s_params, 16)
                sp.dma_start(bg[:, :], b_gate.partition_broadcast(P)).then_inc(s_params, 16)
                for g, t in ((g_xattn, gx), (g_ffn, gf)):
                    sp.dma_start(t[:, :], g.partition_broadcast(P)).then_inc(s_params, 16)

            def load_context(b, p):
                sp.dma_start(ctx_t[p][:, 0:LAST, :],
                             ctx_kv[b, 0:P * LAST, :].rearrange("(a p) d -> p a d", p=P)).then_inc(s_ctx[p], 16)
                first, rows = KV_T[LAST]
                sp.dma_start(ctx_t[p][0:rows, LAST, :], ctx_kv[b, first:KV, :]).then_inc(s_ctx[p], 16)

            def load_weights(e, k, loaded):
                sp.dma_start(raw[:, k, :], w_e[e, k * P:(k + 1) * P, :]).then_inc(loaded, 16)

            def load_bias(e):
                sp.dma_start(bias[:, :], b_e[e, :].partition_broadcast(P)).then_inc(s_bias, 16)

            for b in range(2):
                sp.dma_start(x_all[:, b, :], x[b, :, :]).then_inc(s_x01[b], 16)
                load_context(b, b)
            load_parameters()
            sp.dma_start(x_all[:, 2:B, :], x[2:B, :, :].rearrange("b q d -> q b d")).then_inc(s_x, 16)
            for k in range(KD):
                if k == KD - 1:
                    sp.wait_ge(s_zero, 32)
                load_weights(0, k, s_raw0)

            def step(s, p):
                if isinstance(s, int) and (s == 0 or s > B - 2):
                    return
                sp.wait_ge(s_cl, s)
                sp.wait_ge(s_turned, group(s - 1, KD - 1) + 1)
                load_context(s + 1, 1 - p)

            stage1(sp, step)

            for k in range(KD):
                sp.wait_ge(s_wl0, k + 1)
                load_weights(1, k, s_raw[k])

            sp.wait_ge(s_slot_token, 1)
            sp.wait_ge(s_hstore, 16 * B)
            sp.wait_ge(s_hnstore, 16 * B)
            load_bias(0)

            def weights_of(e, p):
                for k in range(KD):
                    sp.wait_ge(s_wl, KD * (e - 1) + k + 1)
                    load_weights(e + 1, k, s_raw[k])
                sp.wait_ge(s_yev[1], e)
                load_bias(e)

            weights_of(1, 1)
            with sp.Fori(1, E // 2 - 1) as i:
                weights_of(2 * i, 0)
                weights_of(2 * i + 1, 1)
            weights_of(E - 2, 0)
            sp.wait_ge(s_yev[1], E - 1)
            load_bias(E - 1)

        @block.tensor
        def _(pe):
            pe.wait_ge(s_const, 1)

            def turn(s, g, blocks):
                bank = group_bank(s, g)
                n = group(s, g)
                if not isinstance(n, int) or n >= 4:
                    pe.wait_ge(s_evac[g % 2], evacuated(s, g) - 2)
                at = 0
                for rows, src in blocks:
                    mm = nc.tensor.transpose(bank[:, at:at + rows], src, ident[0:rows, 0:rows])
                    at += rows
                mm.then_inc(s_turned, 1)

            def step(s, p):
                has_a, has_b, has_c, _, _ = parts(s)
                if has_a:
                    pe.wait_ge(s_ctx[p], 16 * (s - p) + 32)
                    for g in range(KD):
                        turn(s, g, [(rows, ctx_t[p][0:rows, a, g * P:(g + 1) * P])
                                    for a, (_, rows) in enumerate(KV_T)])
                    pe.wait_ge(s_qn, s + 1)
                    for g in range(2):
                        turn(s, KD + g, [(Q, normed[:, k * P:(k + 1) * P]) for k in range(4 * g, 4 * g + 4)])
                if has_b:
                    pe.wait_ge(s_probs, s)
                    if not isinstance(s, int) or s >= 3:
                        pe.wait_ge(s_acc, s - 2)
                    for a, (first, rows) in enumerate(KV_T):
                        mm = nc.tensor.transpose(probsT_ps[0:rows, a * Q:(a + 1) * Q],
                                                 probs[:, first:first + rows], ident[0:Q, 0:Q])
                    mm.then_inc(s_pT, 1)
                    after(pe, s_h, s - 1)
                    pe.wait_ge(s_pTl, s)
                    pe.wait_ge(s_cl, s)
                    for n in range(2):
                        cols = slice(n * 512, (n + 1) * 512)
                        for a, (_, rows) in enumerate(KV_T):
                            products = ((probsT_h, ctx_h), (probsT_h, ctx_l), (probsT_l, ctx_h))
                            for c, (weights, values) in enumerate(products):
                                mm = nc.tensor.matmul(att_ps[:, cols], weights[0:rows, a, :], values[0:rows, a, cols],
                                                      start=(a == 0 and c == 0), stop=(a == LAST and c == 2))
                    mm.then_inc(s_att, 1)
                if has_c:
                    pe.wait_ge(s_hn, s - 1)
                    for g in range(2):
                        turn(s, NEW + g, [(Q, normed[:, k * P:(k + 1) * P]) for k in range(4 * g, 4 * g + 4)])
                if has_a:
                    pe.wait_ge(s_evac[0], evacuated(s, KD))
                    pe.wait_ge(s_evac[1], evacuated(s, KD + 1))
                    for k in range(KD):
                        mm = nc.tensor.matmul(score_ps, qT[:, k, :], kT[:, k, :], start=(k == 0), stop=(k == KD - 1))
                    mm.then_inc(s_scores, 1)
                if has_c:
                    pe.wait_ge(s_evac[0], evacuated(s, NEW))
                    pe.wait_ge(s_evac[1], evacuated(s, NEW + 1))
                    pe.wait_ge(s_params, 64)
                    for k in range(KD):
                        mm = nc.tensor.matmul(logit_ps, hnT[:, k, :], wg[:, k, :], start=(k == 0), stop=(k == KD - 1))
                    mm.then_inc(s_logit_ps, 1)
                    pe.wait_ge(s_chosen, s - 1)
                    nc.tensor.matmul(rank_ps, before[:, :], chosen[:, :], start=True, stop=False)
                    nc.tensor.matmul(rank_ps, ones[:, :], chosen_sum[:, :], start=False, stop=True).then_inc(s_rank, 1)
                    pe.wait_ge(s_tok_col, s - 1)
                    for c in range(TOP_K):
                        mm = nc.tensor.matmul(slot_ps, at_row[:, c, :], tok_col[:, c, :], start=(c == 0),
                                              stop=(c == TOP_K - 1))
                    mm.then_inc(s_slots_ps, 1)

            stage1(pe, step)
            pe.wait_ge(s_sum, B)
            pe.wait_ge(s_acc, B)
            nc.tensor.matmul(count_ps, ones[:, :], chosen_sum[:, :], start=True, stop=True).then_inc(s_count, 1)

            def turn_rows(t):
                for k in range(KD):
                    mm = nc.tensor.transpose(xT_ps[:, k * P:(k + 1) * P], xg[t][:, k * P:(k + 1) * P], ident[:, :])
                return mm

            def turn_tile(e, t):
                pe.wait_ge(s_gath[t], 16 * e + 16)
                turn_rows(t).then_inc(s_xT[t], 1)

            def multiply(t, p, k, into):
                products = ((xh[t], wh[p]), (xh[t], wl[p]), (xl[t], wh[p]))
                for c, (rows, weights) in enumerate(products):
                    for n in range(2):
                        mm = nc.tensor.matmul(into[:, n * HB:(n + 1) * HB], rows[:, k, :],
                                              weights[:, k, n * HB:(n + 1) * HB],
                                              start=(k == 0 and c == 0), stop=(k == KD - 1 and c == 2))
                return mm

            def expert(e, p, last):
                over = pe.value_load(tile_table[0:1, 0, bass.ds(e, 1)], min_val=0, max_val=OVER)
                over_before = pe.value_load(tile_table[0:1, 1, bass.ds(e, 1)], min_val=0, max_val=OVER * E)
                pe.wait_ge(s_xl[0], e + 1)
                after(pe, s_yev[0], e)
                for k in range(KD):
                    if isinstance(e, int) and e == 0:
                        pe.wait_ge(s_wl0, k + 1)
                    else:
                        pe.wait_ge(s_wl, KD * (e - 1) + k + 1)
                    mm = multiply(0, p, k, y_ps[0])
                    if k == KD // 2:
                        turn_tile(e, 1)
                mm.then_inc(s_mm0, 1)
                with pe.If(over > 0):
                    wait_apart(pe, s_xl[1], e + 1)
                    with pe.Fori(0, OVER) as j:
                        with pe.If(over > j):
                            n = over_before + j
                            pe.wait_ge(o_gath, 16 * n + 16)
                            turn_rows(0).then_inc(o_xT, 1)
                            pe.wait_ge(o_xl, n + 1)
                            pe.wait_ge(o_yev, n + 1)
                            for k in range(KD):
                                mm = multiply(0, p, k, over_ps)
                            mm.then_inc(o_mm, 1)
                pe.wait_ge(s_xl[1], e + 1)
                after(pe, s_yev[1], e)
                for k in range(KD):
                    multiply(1, p, k, y_ps[1]).then_inc(s_wfree, 1)
                    if k == KD // 2 and not last:
                        turn_tile(e + 1, 0)

            pe.wait_ge(s_table, 1)
            turn_tile(0, 0)
            stage3(pe, expert)

        @block.scalar
        def _(act):
            def normalise_queries(b, p):
                act.wait_ge(s_ln, b + 1)
                if not isinstance(b, int) or b >= 3:
                    act.wait_ge(s_turned, group(b - 1, NEW + 1) + 1)
                    act.wait_ge(s_hnstore, 16 * (b - 2))
                elif b > 0:
                    act.wait_ge(s_turned, group(b - 1, KD + 1) + 1)
                nc.scalar.activation(normed[:, :], of_batch(x_all, b), ACT.Identity, bias=shift[p][:, 1:2],
                                     scale=inv_std[p][:, 1:2]).then_inc(s_qn, 1)

            def split_high(k, dst):
                nc.scalar.activation(at_k(dst, k), at_k(raw, k), ACT.Copy).then_inc(s_wh, 1)

            def turned(s, g, dst, cols):
                act.wait_ge(s_turned, group(s, g) + 1)
                nc.scalar.activation(dst, group_bank(s, g)[:, 0:cols], ACT.Copy).then_inc(s_evac[0], 1)

            normalise_queries(0, 0)
            act.wait_ge(s_params, 64)
            nc.scalar.activation(tgx[:, :], gx[:, :], ACT.Tanh).then_inc(s_tanh, 1)
            nc.scalar.activation(tgf[:, :], gf[:, :], ACT.Tanh).then_inc(s_tanh, 1)
            act.wait_ge(s_tanh, 2)
            nc.scalar.mul(tgf_half[:, :], tgf[:, :], 1.0 / TOP_K).then_inc(s_tgf, 1)

            def step(s, p):
                has_a, has_b, has_c, has_next, _ = parts(s)
                if has_a:
                    for g in range(0, KD, 2):
                        turned(s, g, kT[:, g, :], KV)
                    turned(s, KD, qT[:, 0:4, :].rearrange("p k q -> p (k q)"), 4 * Q)
                if has_b:
                    act.wait_ge(s_pT, s)
                    rows = KV_T[LAST][1]
                    nc.scalar.activation(probsT_h[:, 0:LAST, :].rearrange("p a q -> p (a q)"),
                                         probsT_ps[:, 0:LAST * Q], ACT.Copy)
                    nc.scalar.activation(probsT_h[0:rows, LAST, :], probsT_ps[0:rows, LAST * Q:(LAST + 1) * Q],
                                         ACT.Copy).then_inc(s_pTh, 1)
                if has_c:
                    act.wait_ge(s_ln, s + 2)
                    if has_a:
                        act.wait_ge(s_turned, group(s, KD + 1) + 1)
                    else:
                        act.wait_ge(s_turned, group(s - 1, NEW + 1) + 1)
                        act.wait_ge(s_hnstore, 16 * (s - 2))
                    nc.scalar.activation(normed[:, :], of_batch(x_all, s - 2), ACT.Identity, bias=shift[1 - p][:, 0:1],
                                         scale=inv_std[1 - p][:, 0:1]).then_inc(s_hn, 1)
                    turned(s, NEW, hnT[:, 0:4, :].rearrange("p k q -> p (k q)"), 4 * Q)
                if has_a:
                    after(act, s_att, s)
                    for a, (_, rows) in enumerate(KV_T):
                        nc.scalar.activation(ctx_h[0:rows, a, :], ctx_t[p][0:rows, a, :], ACT.Copy).then_inc(s_ch, 1)
                if has_next:
                    normalise_queries(s + 1, 1 - p)
                if has_b:
                    act.wait_ge(s_raw0, 16 * KD)
                    split_high(s - 1, wh[0])
                if has_a:
                    act.wait_ge(s_negmax, s + 1)
                    after(act, s_coef, s)
                    nc.scalar.activation(probs[:, :], score_ps, ACT.Exp, bias=neg_max[:, :],
                                         accum_out=prob_sum[:, :]).then_inc(s_probs, 1)

            stage1(act, step)
            act.wait_ge(s_slot_token, 1)
            act.wait_ge(s_hstore, 16 * B)
            act.wait_ge(s_hnstore, 16 * B)

            def split_rows(t):
                return nc.scalar.activation(xh[t][:, :, :].rearrange("p k m -> p (k m)"), xT_ps[:, :], ACT.Copy)

            def split_tile(e, t):
                act.wait_ge(s_xT[t], e + 1)
                if t == 0:
                    after(act, s_mm0, e)
                else:
                    after(act, s_wfree, KD * e)
                split_rows(t).then_inc(s_xh[t], 1)

            def weights(e, p, ks):
                for k in ks:
                    if not (isinstance(e, int) and e == 1):
                        act.wait_ge(s_wfree, KD * (e - 2) + k + 1)
                    act.wait_ge(s_raw[k], 16 * e)
                    split_high(k, wh[p])

            def expert(e, p, last):
                over = act.value_load(tile_table[0:1, 0, bass.ds(e, 1)], min_val=0, max_val=OVER)
                over_before = act.value_load(tile_table[0:1, 1, bass.ds(e, 1)], min_val=0, max_val=OVER * E)
                if not last:
                    weights(e + 1, 1 - p, range(0, 3))
                split_tile(e, 1)
                if not last:
                    weights(e + 1, 1 - p, range(3, 6))
                with act.If(over > 0):
                    with act.Fori(0, OVER) as j:
                        with act.If(over > j):
                            act.wait_ge(o_xT, over_before + j + 1)
                            split_rows(0).then_inc(o_xh, 1)
                    act.nop()
                if not last:
                    weights(e + 1, 1 - p, range(6, KD))
                    split_tile(e + 1, 0)

            act.wait_ge(s_table, 1)
            split_tile(0, 0)
            stage3(act, expert)

        @block.vector
        def _(dve):
            def statistics(call, h_batch, x_batch, p):
                base = NORM_STEPS * call
                made = [0]

                def link(ins, alone=False):
                    made[0] += 1
                    ins.then_inc(s_norm, 1)
                    if alone:
                        wait_apart(dve, s_norm, base + made[0])
                    else:
                        dve.wait_ge(s_norm, base + made[0])

                batches = (h_batch, x_batch)
                kinds = slice(0 if h_batch is not None else 1, 2 if x_batch is not None else 1)
                for kind in range(kinds.start, kinds.stop):
                    rows = of_batch(x_all, batches[kind])
                    for c in range(2):
                        last = nc.vector.bn_stats(stats[:, kind, c, :], rows[:, c * 512:(c + 1) * 512])
                link(last, True)
                for kind in range(kinds.start, kinds.stop):
                    last = nc.vector.bn_aggr(mean_var[:, kind, :], stats[:, kind, :, :])
                link(last)
                link(nc.vector.tensor_scalar(var_eps[:, kinds], mean_var[:, kinds, 1], EPS, None, ALU.add))
                nc.vector.tensor_scalar(neg_half[:, kinds], var_eps[:, kinds], -0.5, None, ALU.mult)
                link(nc.vector.tensor_scalar(half_bits[:, kinds], var_eps[:, kinds].bitcast(I32), 1, -1,
                                             ALU.logical_shift_right, ALU.bitwise_xor), True)
                link(nc.vector.tensor_tensor(guess[0][:, kinds].bitcast(I32), half_bits[:, kinds],
                                             seed_bits[:, kinds], ALU.add))
                guesses = guess + [inv_std[p]]
                for j in range(NEWTON):
                    r0, r1 = guesses[j][:, kinds], guesses[j + 1][:, kinds]
                    link(nc.vector.tensor_tensor(guess_sq[:, kinds], r0, r0, ALU.mult))
                    link(nc.vector.tensor_tensor(guess_sq[:, kinds], guess_sq[:, kinds], neg_half[:, kinds], ALU.mult))
                    link(nc.vector.scalar_tensor_tensor(out=r1, in0=guess_sq[:, kinds], scalar=1.5, in1=r0,
                                                        op0=ALU.add, op1=ALU.mult))
                assert made[0] == NORM_STEPS
                nc.vector.scalar_tensor_tensor(out=shift[p][:, kinds], in0=mean_var[:, kinds, 0], scalar=-1.0,
                                               in1=inv_std[p][:, kinds], op0=ALU.mult, op1=ALU.mult).then_inc(s_ln, 1)

            def choose(b):
                base = CHOOSE_STEPS * b
                made = [0]

                def link(ins):
                    made[0] += 1
                    ins.then_inc(s_choose, 1)
                    dve.wait_ge(s_choose, base + made[0])

                dve.wait_ge(s_logit_ps, b + 1)
                link(nc.vector.tensor_tensor(logit[:, :], logit_ps, bg[0:Q, :], ALU.add))
                other = logit[:, :].unsqueeze(1).to_broadcast([Q, E, E])
                own = logit[:, :].unsqueeze(2).to_broadcast([Q, E, E])
                nc.vector.tensor_tensor(above[:, :, :], other, own, ALU.is_gt)
                link(nc.vector.tensor_tensor(tied[:, :, :], other, own, ALU.is_equal))
                link(nc.vector.tensor_tensor(tied[:, :, :], tied[:, :, :], lower_e[:, :, :], ALU.mult))
                link(nc.vector.tensor_tensor(above[:, :, :], above[:, :, :], tied[:, :, :], ALU.add))
                link(nc.vector.tensor_reduce(place[:, :], above[:, :, :], AX.X, ALU.add))
                assert made[0] == CHOOSE_STEPS
                nc.vector.tensor_scalar(chosen[:, :], place[:, :], float(TOP_K), None, ALU.is_lt).then_inc(s_chosen, 1)
                nc.vector.tensor_tensor(onehot[:, :, :], place[:, :].unsqueeze(1).to_broadcast([Q, TOP_K, E]),
                                        choice_no[:, :, :], ALU.is_equal).then_inc(s_chosen_own, 1)

            def locate(b):
                base = SLOT_STEPS * b
                made = [0]

                def link(ins):
                    made[0] += 1
                    ins.then_inc(s_slot, 1)
                    dve.wait_ge(s_slot, base + made[0])

                dve.wait_ge(s_rank, b + 1)
                link(nc.vector.tensor_tensor(slot_of[:, :], rank_ps, expert_base[:, :], ALU.add))
                dve.wait_ge(s_chosen_own, b + 1)
                link(nc.vector.tensor_tensor(picked[:, :, :], slot_of[:, :].unsqueeze(1).to_broadcast([Q, TOP_K, E]),
                                             onehot[:, :, :], ALU.mult))
                with nc.allow_low_precision(reason="whole numbers below 2**13"):
                    link(nc.vector.tensor_reduce(slot_i[:, :], picked[:, :, :], AX.X, ALU.add))
                nc.vector.tensor_scalar(slot_col_i[:, :], slot_i[:, :], 7, None, ALU.logical_shift_right)
                link(nc.vector.tensor_scalar(slot_row_i[:, :], slot_i[:, :], P - 1, None, ALU.bitwise_and))
                nc.vector.tensor_copy(slot_col[:, :], slot_col_i[:, :])
                link(nc.vector.tensor_copy(slot_row[:, :], slot_row_i[:, :]))
                assert made[0] == SLOT_STEPS
                for c in range(TOP_K):
                    nc.vector.tensor_scalar(at_row[:, c, :], iota_slot[:, :], slot_row[:, c:c + 1], None, ALU.is_equal)
                    last = nc.vector.tensor_scalar(tok_col[:, c, :], iota_col[:, :], slot_col[:, c:c + 1],
                                                   tok_far[:, bass.ds(b, 1)], ALU.is_equal, ALU.mult)
                last.then_inc(s_tok_col, 1)
                nc.vector.tensor_tensor(chosen_sum[:, :], chosen_sum[:, :], chosen[:, :], ALU.add).then_inc(s_sum, 1)

            def add_slots(b):
                dve.wait_ge(s_slots_ps, b + 1)
                after(dve, s_acc, b)
                nc.vector.tensor_tensor(slot_acc[:, :], slot_acc[:, :], slot_ps, ALU.add).then_inc(s_acc, 1)

            def turned(s, g, dst, cols):
                dve.wait_ge(s_turned, group(s, g) + 1)
                nc.vector.tensor_copy(dst, group_bank(s, g)[:, 0:cols]).then_inc(s_evac[1], 1)

            dve.wait_ge(s_const, 1)
            for b in range(2):
                dve.wait_ge(s_x01[b], 16)
                statistics(b, None, b, b)
            dve.wait_ge(s_tanh, 2)

            def step(s, p):
                has_a, has_b, has_c, _, has_next2 = parts(s)
                if has_a:
                    for g in range(1, KD, 2):
                        turned(s, g, kT[:, g, :], KV)
                    turned(s, KD + 1, qT[:, 4:8, :].rearrange("p k q -> p (k q)"), 4 * Q)
                if has_b:
                    dve.wait_ge(s_probs, s)
                    nc.vector.reciprocal(inv_sum[:, :], prob_sum[:, :]).then_inc(s_inv, 1)
                    dve.wait_ge(s_pTh, s)
                    rows = KV_T[LAST][1]
                    nc.vector.tensor_tensor(probsT_l[:, 0:LAST, :].rearrange("p a q -> p (a q)"), probsT_ps[:, 0:LAST * Q],
                                            probsT_h[:, 0:LAST, :].rearrange("p a q -> p (a q)"), ALU.subtract)
                    nc.vector.tensor_tensor(probsT_l[0:rows, LAST, :], probsT_ps[0:rows, LAST * Q:(LAST + 1) * Q],
                                            probsT_h[0:rows, LAST, :], ALU.subtract).then_inc(s_pTl, 1)
                    dve.wait_ge(s_inv, s)
                    nc.vector.tensor_tensor(coef[:, :], inv_sum[:, :], tgx[0:Q, :], ALU.mult).then_inc(s_coef, 1)
                if has_c:
                    turned(s, NEW + 1, hnT[:, 4:8, :].rearrange("p k q -> p (k q)"), 4 * Q)
                if has_b:
                    dve.wait_ge(s_coef, s)
                    dve.wait_ge(s_att, s)
                    rows = of_batch(x_all, s - 1)
                    nc.vector.scalar_tensor_tensor(out=rows, in0=att_ps, scalar=coef[:, 0:1], in1=rows,
                                                   op0=ALU.mult, op1=ALU.add).then_inc(s_h, 1)
                if has_b or has_next2:
                    if has_b:
                        wait_apart(dve, s_h, s)
                    if isinstance(s, int) and s == 0:
                        dve.wait_ge(s_x, 16)
                    if has_a:
                        dve.wait_ge(s_qn, s + 1 if not isinstance(s, int) else min(s + 1, B))
                    if not isinstance(s, int) or s >= 3:
                        wait_apart(dve, s_hn, s - 2)
                    statistics(s + 2, s - 1 if has_b else None, s + 2 if has_next2 else None, p)
                if has_a:
                    dve.wait_ge(s_scores, s + 1)
                    after(dve, s_probs, s)
                    nc.vector.tensor_reduce(neg_max[:, :], score_ps, AX.X, ALU.max, negate=True).then_inc(s_negmax, 1)
                if has_c:
                    choose(s - 2)
                    locate(s - 2)
                    add_slots(s - 2)

            def split_low(e, k, p):
                dve.wait_ge(s_wh, KD * (e + 1) + k + 1)
                nc.vector.tensor_tensor(at_k(wl[p], k), at_k(raw, k), at_k(wh[p], k), ALU.subtract).then_inc(s_wl, 1)

            stage1(dve, step)

            made = [0]

            def link(ins):
                made[0] += 1
                ins.then_inc(s_last, 1)
                dve.wait_ge(s_last, made[0])

            dve.wait_ge(s_acc, B)
            link(nc.vector.tensor_scalar(used[:, :], slot_acc[:, :], 0.0, used_shift[:, 0:1], ALU.is_lt, ALU.mult))
            nc.vector.scalar_tensor_tensor(out=slot_token[:, :], in0=slot_acc[:, :], scalar=spare_row[:, 0:1],
                                           in1=used[:, :], op0=ALU.add, op1=ALU.add).then_inc(s_slot_token, 1)
            dve.wait_ge(s_count, 1)
            link(nc.vector.tensor_scalar(over_f[:, :], count_ps[0:1, :], float(-STATIC_TILES * P + P - 1), 0.0,
                                         ALU.add, ALU.max))
            link(nc.vector.tensor_copy(over_i[:, :], over_f[:, :]))
            link(nc.vector.tensor_scalar(tile_table[:, 0, :], over_i[:, :], 7, None, ALU.logical_shift_right))
            link(nc.vector.tensor_copy(over_e[:, :], tile_table[:, 0, :]))
            link(nc.vector.tensor_tensor(over_m[:, :, :], lower_e[0:1, :, :],
                                         over_e[:, :].unsqueeze(1).to_broadcast([1, E, E]), ALU.mult))
            link(nc.vector.tensor_reduce(over_b[:, :], over_m[:, :, :], AX.X, ALU.add))
            nc.vector.tensor_copy(tile_table[:, 1, :], over_b[:, :]).then_inc(s_table, 1)
            dve.wait_ge(s_hstore, 16 * B)
            dve.wait_ge(s_hnstore, 16 * B)

            dve.wait_ge(s_tgf, 1)
            dve.nop().then_inc(o_yev, 1)

            def split_rows(t):
                return nc.vector.tensor_tensor(xl[t][:, :, :].rearrange("p k m -> p (k m)"), xT_ps[:, :],
                                               xh[t][:, :, :].rearrange("p k m -> p (k m)"), ALU.subtract)

            def split_tile(e, t):
                dve.wait_ge(s_xh[t], e + 1)
                split_rows(t).then_inc(s_xl[t], 1)

            def weights(e, p, ks):
                for k in ks:
                    split_low(e - 1, k, p)

            def finish(banks, dst, evacuated_sem, n, ready):
                nc.vector.tensor_tensor(dst[:, :], banks[:, :], bias[:, :], ALU.add).then_inc(evacuated_sem, 1)
                dve.wait_ge(evacuated_sem, n)
                nc.vector.tensor_scalar(dst[:, :], dst[:, :], 0.0, tgf_half[:, 0:1], ALU.max, ALU.mult
                                        ).then_inc(ready, 1)

            def evacuate(e, t):
                if t == 0:
                    dve.wait_ge(s_mm0, e + 1)
                else:
                    dve.wait_ge(s_wfree, KD * e + KD)
                dve.wait_ge(s_bias, 16 * e + 16)
                if not (isinstance(e, int) and e == 0):
                    dve.wait_ge(s_added, 16 * (2 * e + t - 1))
                finish(y_ps[t], y[t], s_yev[t], e + 1, s_y)

            def expert(e, p, last):
                over = dve.value_load(tile_table[0:1, 0, bass.ds(e, 1)], min_val=0, max_val=OVER)
                over_before = dve.value_load(tile_table[0:1, 1, bass.ds(e, 1)], min_val=0, max_val=OVER * E)
                if not last:
                    weights(e + 1, 1 - p, range(0, 3))
                split_tile(e, 1)
                if not last:
                    weights(e + 1, 1 - p, range(3, 6))
                evacuate(e, 0)
                with dve.If(over > 0):
                    with dve.Fori(0, OVER) as j:
                        with dve.If(over > j):
                            n = over_before + j
                            dve.wait_ge(o_xh, n + 1)
                            split_rows(0).then_inc(o_xl, 1)
                            dve.wait_ge(o_mm, n + 1)
                            dve.wait_ge(o_free, n + 1)
                            finish(over_ps, y_over, o_yev, n + 2, o_y)
                    dve.nop()
                if not last:
                    weights(e + 1, 1 - p, range(6, KD))
                    split_tile(e + 1, 0)
                evacuate(e, 1)

            split_tile(0, 0)
            stage3(dve, expert)

        @block.gpsimd
        def _(pool):
            made = [0]

            def link(ins):
                made[0] += 1
                ins.then_inc(s_const0, 1)
                return made[0]

            g = nc.gpsimd
            link(g.memset(ident[:, :], 0.0))
            link(g.memset(before[:, :], 1.0))
            link(g.memset(lower_e[:, :, :], 1.0))
            link(g.memset(raw[:, KD - 1, :], 0.0))
            link(g.iota(seed_bits[:, :], [[0, 2]], base=SEED_BITS, channel_multiplier=0))
            link(g.memset(ones[:, :], 1.0))
            link(g.memset(chosen_sum[:, :], 0.0))
            link(g.memset(slot_acc[:, :], 0.0))
            link(g.iota(choice_no[:, :, :], [[1, TOP_K], [0, E]], base=0, channel_multiplier=0,
                        allow_small_or_imprecise_dtypes=True))
            link(g.iota(iota_slot[:, :], [[1, P]], base=0, channel_multiplier=0, allow_small_or_imprecise_dtypes=True))
            link(g.iota(iota_col[:, :], [[1, COLS]], base=0, channel_multiplier=0, allow_small_or_imprecise_dtypes=True))
            link(g.iota(expert_base[:, :], [[MAX_TILES * P, E]], base=0, channel_multiplier=0,
                        allow_small_or_imprecise_dtypes=True))
            link(g.iota(tok_far[:, :], [[Q, B]], base=-FAR, channel_multiplier=1, allow_small_or_imprecise_dtypes=True))
            link(g.iota(spare_row[:, :], [[0, 1]], base=N_TOK, channel_multiplier=1, allow_small_or_imprecise_dtypes=True))
            link(g.iota(used_shift[:, :], [[0, 1]], base=FAR - N_TOK, channel_multiplier=-1,
                        allow_small_or_imprecise_dtypes=True))
            pool.wait_ge(s_const0, made[0])
            link(g.affine_select(out=ident[:, :], in_=ident[:, :], compare_op=ALU.not_equal, fill=1.0, base=0,
                                 pattern=[[-1, P]], channel_multiplier=1))
            link(g.affine_select(out=before[:, :], in_=before[:, :], compare_op=ALU.is_gt, fill=0.0, base=0,
                                 pattern=[[1, Q]], channel_multiplier=-1))
            link(g.affine_select(out=lower_e[:, :, :], in_=lower_e[:, :, :], compare_op=ALU.is_gt, fill=0.0, base=0,
                                 pattern=[[1, E], [-1, E]], channel_multiplier=0))
            pool.wait_ge(s_const0, made[0])
            pool.nop().then_inc(s_const, 1)
            for rows in (out, hn_rows):
                g.dma_start(rows[N_TOK:N_TOK + P, :], raw[:, KD - 1, :]).then_inc(s_zero, 16)

            def step(s, p):
                has_a, has_b, has_c, _, _ = parts(s)
                if has_c:
                    wait_apart(pool, s_hn, s - 1)
                    g.dma_start(hn_rows[bass.ds((s - 2) * Q, Q), :], normed[:, :]).then_inc(s_hnstore, 16)
                if has_b:
                    wait_apart(pool, s_h, s)
                    g.dma_start(out[bass.ds((s - 1) * Q, Q), :], of_batch(x_all, s - 1)).then_inc(s_hstore, 16)
                if has_a:
                    for a, (_, rows) in enumerate(KV_T):
                        pool.wait_ge(s_ch, 3 * s + a + 1)
                        last = g.tensor_tensor(ctx_l[0:rows, a, :], ctx_t[p][0:rows, a, :], ctx_h[0:rows, a, :],
                                               ALU.subtract)
                    last.then_inc(s_cl, 1)
                if has_b:
                    pool.wait_ge(s_wh, s)
                    g.tensor_tensor(at_k(wl[0], s - 1), at_k(raw, s - 1), at_k(wh[0], s - 1),
                                    ALU.subtract).then_inc(s_wl0, 1)

            stage1(pool, step)

            pool.wait_ge(s_slot_token, 1)
            pool.wait_ge(s_zero, 32)
            pool.wait_ge(s_hstore, 16 * B)
            pool.wait_ge(s_hnstore, 16 * B)

            def gather(dst, idx, done_sem):
                g.indirect_dma_start(dst[:, :], None, hn_rows, bass.IndirectOffsetOnAxis(idx, 0)).then_inc(done_sem, 16)

            def gather_tile(e, t, p):
                idx = idx_now[:, 2 * p + t:2 * p + t + 1]
                if not (isinstance(e, int) and e == 0):
                    pool.wait_ge(s_xT[t], e)
                if not (isinstance(e, int) and e < 2):
                    pool.wait_ge(s_added, 32 * (e - 2) + 16 * t + 16)
                g.tensor_copy(idx, slot_token[:, bass.ds(e * MAX_TILES + t, 1)]).then_inc(s_idx, 1)
                wait_apart(pool, s_idx, 2 * e + t + 1)
                gather(xg[t], idx, s_gath[t])

            def add_rows(rows, idx, added):
                g.indirect_dma_start(out, bass.IndirectOffsetOnAxis(idx, 0), rows[:, :], None,
                                     compute_op=ALU.add).then_inc(added, 16)

            def add_tile(e, t, p):
                pool.wait_ge(s_y, 2 * e + t + 1)
                if not (isinstance(e, int) and e == 0 and t == 0):
                    wait_apart(pool, s_added, 16 * (2 * e + t))
                add_rows(y[t], idx_now[:, 2 * p + t:2 * p + t + 1], s_added)

            def expert(e, p, last):
                over = pool.value_load(tile_table[0:1, 0, bass.ds(e, 1)], min_val=0, max_val=OVER)
                over_before = pool.value_load(tile_table[0:1, 1, bass.ds(e, 1)], min_val=0, max_val=OVER * E)
                with pool.If(over > 0):
                    pool.wait_ge(s_xT[0], e + 1)
                    wait_apart(pool, s_added, 32 * e)
                    idx = idx_now[:, 2 * STATIC_TILES:2 * STATIC_TILES + 1]
                    with pool.Fori(0, OVER) as j:
                        with pool.If(over > j):
                            n = over_before + j
                            g.tensor_copy(idx, slot_token[:, bass.ds(e * MAX_TILES + STATIC_TILES + j, 1)]).then_inc(o_idx, 1)
                            wait_apart(pool, o_idx, n + 1)
                            gather(xg[0], idx, o_gath)
                            wait_apart(pool, o_y, n + 1)
                            add_rows(y_over, idx, o_added)
                            pool.wait_ge(o_added, 16 * n + 16)
                            pool.nop().then_inc(o_free, 1)
                    pool.nop()
                if not last:
                    gather_tile(e + 1, 0, 1 - p)
                    gather_tile(e + 1, 1, 1 - p)
                add_tile(e, 0, p)
                add_tile(e, 1, p)

            gather_tile(0, 0, 0)
            gather_tile(0, 1, 0)
            pool.wait_ge(s_table, 1)
            pool.nop().then_inc(o_free, 1)
            stage3(pool, expert)
            pool.wait_ge(s_added, 16 * 2 * E)


NEWTON = 3
SEED_BITS = 0x5F3759DF + 1
NORM_STEPS = 5 + 3 * NEWTON

CHOOSE_STEPS = 5
SLOT_STEPS = 5

_INS = ["x", "ctx_4096", "g_xattn", "g_ffn", "L0_ffn_W_gate", "L0_ffn_b_gate", "L0_ffn_W_e", "L0_ffn_b_e"]


def kernel(**inputs):
    import numpy as np
    import concourse.bacc as bacc
    from concourse.bass_utils import run_bass_kernel_spmd

    nc = bacc.Bacc("TRN2", target_bir_lowering=False, num_devices=1)
    arrays, args = {}, []
    for name in _INS:
        a = np.ascontiguousarray(inputs[name])
        arrays[f"in_{name}"] = a
        args.append(nc.dram_tensor(f"in_{name}", a.shape, mybir.dt.from_np(a.dtype), kind="ExternalInput").ap())
    b, q, d = inputs["x"].shape
    out = nc.dram_tensor("out_rows", [b * q + P, d], F32, kind="ExternalOutput").ap()
    gated_block(nc, *args, out)
    r = run_bass_kernel_spmd(nc, [arrays], core_ids=[0])
    return r.results[0]["out_rows"][:b * q].reshape(b, q, d)
```

```python
from contextlib import ExitStack

import concourse.bass as bass
from concourse import mybir

F32 = mybir.dt.float32
F32R = mybir.dt.float32r
F16 = mybir.dt.float16
I32 = mybir.dt.int32
ALU = mybir.AluOpType
ACT = mybir.ActivationFunctionType
AX = mybir.AxisListType

P = 128
EPS = 1e-5
TOP_K = 2
STATIC_TILES = 2
FAR = 1000


def gated_block(nc, x, ctx_kv, g_xattn, g_ffn, w_gate, b_gate, w_e, b_e, out):
    B, Q, D = x.shape
    KV = ctx_kv.shape[1]
    E = w_gate.shape[1]
    H = w_e.shape[2]
    KD = D // P
    HB = H // 2
    N_TOK = B * Q
    KV_T = [(a, min(P, KV - a)) for a in range(0, KV, P)]
    LAST = len(KV_T) - 1
    MAX_TILES = -(-N_TOK // P)
    OVER = MAX_TILES - STATIC_TILES
    COLS = E * MAX_TILES
    assert out.shape[0] == N_TOK + P and H == D and E == KD and B % 2 == 0 and E % 2 == 0
    assert N_TOK < FAR

    es = ExitStack()
    with es:
        def sb(name, shape, dt=F32, stack=es):
            return stack.enter_context(nc.sbuf_tensor(name, shape, dt))

        def sem(name):
            return es.enter_context(nc.semaphore(name))

        hn_rows = nc.dram_tensor("hn_rows", [N_TOK + P, D], F32, kind="Internal").ap()

        ident = sb("ident", [P, P])
        before = sb("before", [Q, Q], F16)
        ones = sb("ones", [Q, Q], F16)
        iota_slot = sb("iota_slot", [Q, P])
        iota_col = sb("iota_col", [Q, COLS])
        expert_base = sb("expert_base", [Q, E])
        choice_no = sb("choice_no", [Q, TOP_K, E])
        tok_far = sb("tok_far", [Q, B])
        spare_row = sb("spare_row", [P, 1])
        used_shift = sb("used_shift", [P, 1])
        seed_bits = sb("seed_bits", [Q, B], I32)
        lower_e = sb("lower_e", [Q, E, E])
        wg = sb("wg", [P, KD, E])
        bg = sb("bg", [P, E])
        gx = sb("gx", [P, 1])
        gf = sb("gf", [P, 1])
        tgx = sb("tgx", [P, 1])
        tgf = sb("tgf", [P, 1])
        tgf_half = sb("tgf_half", [P, 1])
        tile_table = sb("tile_table", [1, 2, E], I32)
        slot_token = sb("slot_token", [P, COLS], I32)
        idx_now = sb("idx_now", [P, 2 * STATIC_TILES + 1], I32)

        raw = sb("raw", [P, KD, H])
        wh = [sb("wh0", [P, KD, H], F32R), None]
        wl = [sb("wl0", [P, KD, H], F32R), None]

        att = ExitStack()
        ctx_t = [sb(f"ctx{p}", [P, len(KV_T), D], stack=att) for p in range(2)]
        ctx_h = sb("ctx_h", [P, len(KV_T), D], F32R, stack=att)
        ctx_l = sb("ctx_l", [P, len(KV_T), D], F32R, stack=att)
        kT = sb("kT", [P, KD, KV], stack=att)
        x_all = sb("x_all", [Q, B, D], stack=att)
        normed = sb("normed", [Q, D], stack=att)
        qT = sb("qT", [P, KD, Q], stack=att)
        probs = sb("probs", [Q, KV], stack=att)
        probsT_h = sb("probsT_h", [P, len(KV_T), Q], F32R, stack=att)
        probsT_l = sb("probsT_l", [P, len(KV_T), Q], F32R, stack=att)
        hnT = sb("hnT", [P, KD, Q], stack=att)
        stats = sb("stats", [Q, B, 2, 6], stack=att)
        mean_var = sb("mean_var", [Q, B, 2], stack=att)
        var_eps = sb("var_eps", [Q, B], stack=att)
        neg_half = sb("neg_half", [Q, B], stack=att)
        half_bits = sb("half_bits", [Q, B], I32, stack=att)
        guess = [sb(f"guess{j}", [Q, B], stack=att) for j in range(NEWTON)]
        guess_sq = sb("guess_sq", [Q, B], stack=att)
        inv_std = sb("inv_std", [Q, B + 1], stack=att)
        shift = sb("shift", [Q, B + 1], stack=att)
        neg_max = sb("neg_max", [Q, 1], stack=att)
        prob_sum = sb("prob_sum", [Q, 1], stack=att)
        inv_sum = sb("inv_sum", [Q, 1], stack=att)
        coef = sb("coef", [Q, 1], stack=att)
        logit = sb("logit", [Q, E], stack=att)
        above = sb("above", [Q, E, E], stack=att)
        tied = sb("tied", [Q, E, E], stack=att)
        place = sb("place", [Q, E], stack=att)
        onehot = sb("onehot", [Q, TOP_K, E], stack=att)
        chosen = sb("chosen", [Q, E], F16, stack=att)
        chosen_sum = sb("chosen_sum", [Q, E], F16, stack=att)
        slot_of = sb("slot_of", [Q, E], stack=att)
        picked = sb("picked", [Q, TOP_K, E], stack=att)
        slot_i = sb("slot_i", [Q, TOP_K], I32, stack=att)
        slot_col_i = sb("slot_col_i", [Q, TOP_K], I32, stack=att)
        slot_row_i = sb("slot_row_i", [Q, TOP_K], I32, stack=att)
        slot_col = sb("slot_col", [Q, TOP_K], stack=att)
        slot_row = sb("slot_row", [Q, TOP_K], stack=att)
        at_row = sb("at_row", [Q, TOP_K, P], F16, stack=att)
        tok_col = sb("tok_col", [Q, TOP_K, COLS], F16, stack=att)
        slot_acc = sb("slot_acc", [P, COLS], stack=att)
        used = sb("used", [P, COLS], stack=att)
        over_f = sb("over_f", [1, E], stack=att)
        over_i = sb("over_i", [1, E], I32, stack=att)
        over_e = sb("over_e", [1, E], stack=att)
        over_m = sb("over_m", [1, E, E], stack=att)
        over_b = sb("over_b", [1, E], stack=att)
        att.close()

        wh[1] = sb("wh1", [P, KD, H], F32R)
        wl[1] = sb("wl1", [P, KD, H], F32R)
        xg = [sb(f"xg{t}", [P, D]) for t in range(2)]
        xh = [sb(f"xh{t}", [P, KD, P], F32R) for t in range(2)]
        xl = [sb(f"xl{t}", [P, KD, P], F32R) for t in range(2)]
        y = [sb(f"y{t}", [P, H]) for t in range(2)]
        y_over = sb("y_over", [P, H])
        bias = sb("bias", [P, H])

        ps = [es.enter_context(nc.psum_tensor(f"ps{j}", [P, 2 * 512], F32)) for j in range(4)]
        turn_bank = [ps[j // 2][:, 512 * (j % 2):512 * (j % 2) + 512] for j in range(4)]
        score_ps = ps[2][0:Q, 0:KV]
        rank_ps = ps[2][0:Q, 368:368 + E]
        slot_ps = ps[2][:, 384:384 + COLS]
        count_ps = ps[2][0:Q, 448:448 + E]
        probsT_ps = ps[2][:, 512:512 + len(KV_T) * Q]
        logit_ps = ps[2][0:Q, 840:840 + E]
        att_ps = ps[3][0:Q, 0:D]
        xT_ps, over_ps, *y_ps = ps

        s_params = sem("params_loaded")
        s_const0 = sem("const_filled")
        s_const = sem("const_ready")
        s_tanh = sem("tanh_ready")
        s_tgf = sem("tgf_half_ready")
        s_zero = sem("spare_rows_zeroed")
        s_x0 = sem("x0_loaded")
        s_x = sem("x_rest_loaded")
        s_ctx = [sem(f"ctx_loaded{p}") for p in range(2)]
        s_raw0 = sem("raw_loaded_first")
        s_raw = [sem(f"raw_loaded{k}") for k in range(KD)]
        s_turned = sem("turned")
        s_evac = [sem("evac_act"), sem("evac_dve")]
        s_norm = sem("norm_step")
        s_xln = sem("x_norm_ready")
        s_hln = sem("h_norm_ready")
        s_qn = sem("qn_ready")
        s_scores = sem("scores_ready")
        s_negmax = sem("neg_max_ready")
        s_probs = sem("probs_ready")
        s_inv = sem("inv_sum_ready")
        s_coef = sem("coef_ready")
        s_pT = sem("probs_turned")
        s_pTh = sem("probsT_high_ready")
        s_pTl = sem("probsT_low_ready")
        s_ch = sem("ctx_high_ready")
        s_cl = sem("ctx_low_ready")
        s_att = sem("attention_ready")
        s_h = sem("h_ready")
        s_hn = sem("hn_ready")
        s_logit_ps = sem("logits_multiplied")
        s_hstore = sem("h_stored")
        s_hnstore = sem("hn_stored")
        s_wh = sem("w_high_ready")
        s_wl = sem("w_low_ready")
        s_wl0 = sem("w_low_ready_first")
        s_wfree = sem("w_used")
        s_chosen = sem("chosen_ready")
        s_chosen_own = sem("onehot_ready")
        s_rank = sem("ranks_ready")
        s_sum = sem("chosen_summed")
        s_slot = sem("slot_step")
        s_tok_col = sem("tok_col_ready")
        s_slots_ps = sem("slots_ready")
        s_acc = sem("slots_added")
        s_count = sem("counts_ready")
        s_last = sem("table_step")
        s_table = sem("tile_table_ready")
        s_slot_token = sem("slot_token_ready")
        s_bias = sem("bias_loaded")
        s_idx = sem("idx_staged")
        s_gath = [sem(f"gathered{t}") for t in range(2)]
        s_xT = [sem(f"x_turned{t}") for t in range(2)]
        s_xh = [sem(f"x_high_ready{t}") for t in range(2)]
        s_xl = [sem(f"x_low_ready{t}") for t in range(2)]
        s_mm0 = sem("tile0_multiplied")
        s_yev = [sem(f"y_evacuated{t}") for t in range(2)]
        s_y = sem("y_ready")
        s_added = sem("y_added")
        o_idx = sem("over_idx_staged")
        o_gath = sem("over_gathered")
        o_xT = sem("over_x_turned")
        o_xh = sem("over_x_high_ready")
        o_xl = sem("over_x_low_ready")
        o_mm = sem("over_multiplied")
        o_yev = sem("over_y_evacuated")
        o_y = sem("over_y_ready")
        o_added = sem("over_y_added")
        o_free = sem("over_y_free")

        def wait_apart(eng, semaphore, value):
            if not isinstance(value, int):
                value = eng.to_reg(value)
            eng.wait_ge(s_const, 1)
            eng.wait_ge(semaphore, value)

        def of_batch(tile, b):
            return tile[:, bass.ds(b, 1), :].rearrange("q a n -> q (a n)")

        def at_k(tile, k):
            return tile[:, bass.ds(k, 1), :].rearrange("p a n -> p (a n)")

        def after(eng, semaphore, value):
            if not (isinstance(value, int) and value == 0):
                eng.wait_ge(semaphore, value)

        def stage1(eng, step):
            for s in range(3):
                step(s, s % 2)
            with eng.Fori(1, B // 2 - 1) as i:
                step(2 * i + 1, 1)
                step(2 * i + 2, 0)
            for s in range(B - 1, B + 3):
                step(s, s % 2)

        def parts(s):
            if not isinstance(s, int):
                return True, True, True, True
            return s < B, 1 <= s <= B, 2 <= s <= B + 1, s >= 3

        def stage3(eng, expert):
            expert(0, 0, False)
            expert(1, 1, False)
            with eng.Fori(1, E // 2 - 1) as i:
                expert(2 * i, 0, False)
                expert(2 * i + 1, 1, False)
            expert(E - 2, 0, False)
            expert(E - 1, 1, True)

        NEW = KD + 2
        GROUPS = NEW + 2

        def group(s, g):
            if not isinstance(s, int):
                return GROUPS * s - 4 + g
            before_s = sum(NEW * (c < B) + 2 * (2 <= c <= B + 1) for c in range(s))
            return before_s + (g if s < B else g - NEW)

        def group_bank(s, g):
            return turn_bank[(group(s, g) if isinstance(s, int) else g) % 4]

        def evacuated(s, g):
            if not isinstance(s, int):
                return GROUPS // 2 * s - 2 + g // 2 + 1
            return group(s, g) // 2 + 1

        block = es.enter_context(nc.Block())

        @block.sync
        def _(sp):
            def load_parameters():
                sp.dma_start(wg[:, :, :], w_gate.rearrange("(k p) e -> p k e", p=P)).then_inc(s_params, 16)
                sp.dma_start(bg[:, :], b_gate.partition_broadcast(P)).then_inc(s_params, 16)
                for g, t in ((g_xattn, gx), (g_ffn, gf)):
                    sp.dma_start(t[:, :], g.partition_broadcast(P)).then_inc(s_params, 16)

            def load_context(b, p):
                sp.dma_start(ctx_t[p][:, 0:LAST, :],
                             ctx_kv[b, 0:P * LAST, :].rearrange("(a p) d -> p a d", p=P)).then_inc(s_ctx[p], 16)
                first, rows = KV_T[LAST]
                sp.dma_start(ctx_t[p][0:rows, LAST, :], ctx_kv[b, first:KV, :]).then_inc(s_ctx[p], 16)

            def load_weights(e, k, loaded):
                sp.dma_start(raw[:, k, :], w_e[e, k * P:(k + 1) * P, :]).then_inc(loaded, 16)

            def load_bias(e):
                sp.dma_start(bias[:, :], b_e[e, :].partition_broadcast(P)).then_inc(s_bias, 16)

            sp.dma_start(x_all[:, 0, :], x[0, :, :]).then_inc(s_x0, 16)
            load_context(0, 0)
            sp.dma_start(x_all[:, 1:B, :], x[1:B, :, :].rearrange("b q d -> q b d")).then_inc(s_x, 16)
            load_context(1, 1)
            load_parameters()
            for k in range(KD):
                if k == KD - 1:
                    sp.wait_ge(s_zero, 32)
                load_weights(0, k, s_raw0)

            def step(s, p):
                if isinstance(s, int) and (s == 0 or s > B - 2):
                    return
                sp.wait_ge(s_cl, s)
                sp.wait_ge(s_turned, group(s - 1, KD - 1) + 1)
                load_context(s + 1, 1 - p)

            stage1(sp, step)

            for k in range(KD):
                sp.wait_ge(s_wl0, k + 1)
                load_weights(1, k, s_raw[k])

            sp.wait_ge(s_slot_token, 1)
            sp.wait_ge(s_hstore, 16 * B)
            sp.wait_ge(s_hnstore, 16 * B)
            load_bias(0)

            def weights_of(e, p):
                for k in range(KD):
                    sp.wait_ge(s_wl, KD * (e - 1) + k + 1)
                    load_weights(e + 1, k, s_raw[k])
                sp.wait_ge(s_yev[1], e)
                load_bias(e)

            weights_of(1, 1)
            with sp.Fori(1, E // 2 - 1) as i:
                weights_of(2 * i, 0)
                weights_of(2 * i + 1, 1)
            weights_of(E - 2, 0)
            sp.wait_ge(s_yev[1], E - 1)
            load_bias(E - 1)

        @block.tensor
        def _(pe):
            pe.wait_ge(s_const, 1)

            def turn(s, g, blocks):
                bank = group_bank(s, g)
                n = group(s, g)
                if not isinstance(n, int) or n >= 4:
                    pe.wait_ge(s_evac[g % 2], evacuated(s, g) - 2)
                at = 0
                for rows, src in blocks:
                    mm = nc.tensor.transpose(bank[:, at:at + rows], src, ident[0:rows, 0:rows])
                    at += rows
                mm.then_inc(s_turned, 1)

            def step(s, p):
                has_a, has_b, has_c, has_d = parts(s)

                def turn_context(groups):
                    for g in groups:
                        turn(s, g, [(rows, ctx_t[p][0:rows, a, g * P:(g + 1) * P])
                                    for a, (_, rows) in enumerate(KV_T)])

                if has_a:
                    pe.wait_ge(s_ctx[p], 16 * (s - p) + 32)
                    turn_context(range(0, KD - 2))
                if has_b:
                    pe.wait_ge(s_probs, s)
                    if has_d:
                        pe.wait_ge(s_chosen, s - 2)
                    for a, (first, rows) in enumerate(KV_T):
                        mm = nc.tensor.transpose(probsT_ps[0:rows, a * Q:(a + 1) * Q],
                                                 probs[:, first:first + rows], ident[0:Q, 0:Q])
                    mm.then_inc(s_pT, 1)
                if has_d:
                    pe.wait_ge(s_chosen, s - 2)
                    if not isinstance(s, int) or s > 3:
                        pe.wait_ge(s_sum, s - 3)
                    nc.tensor.matmul(rank_ps, before[:, :], chosen[:, :], start=True, stop=False)
                    nc.tensor.matmul(rank_ps, ones[:, :], chosen_sum[:, :], start=False, stop=True).then_inc(s_rank, 1)
                if has_a:
                    turn_context(range(KD - 2, KD))
                    pe.wait_ge(s_qn, s + 1)
                    for g in range(2):
                        turn(s, KD + g, [(Q, normed[:, k * P:(k + 1) * P]) for k in range(4 * g, 4 * g + 4)])
                if has_b:
                    after(pe, s_h, s - 1)
                    pe.wait_ge(s_pTl, s)
                    pe.wait_ge(s_cl, s)
                    for n in range(2):
                        cols = slice(n * 512, (n + 1) * 512)
                        for a, (_, rows) in enumerate(KV_T):
                            products = ((probsT_h, ctx_h), (probsT_h, ctx_l), (probsT_l, ctx_h))
                            for c, (weights, values) in enumerate(products):
                                mm = nc.tensor.matmul(att_ps[:, cols], weights[0:rows, a, :], values[0:rows, a, cols],
                                                      start=(a == 0 and c == 0), stop=(a == LAST and c == 2))
                    mm.then_inc(s_att, 1)
                if has_d:
                    pe.wait_ge(s_tok_col, s - 2)
                    for c in range(TOP_K):
                        mm = nc.tensor.matmul(slot_ps, at_row[:, c, :], tok_col[:, c, :], start=(c == 0),
                                              stop=(c == TOP_K - 1))
                    mm.then_inc(s_slots_ps, 1)
                if has_c:
                    pe.wait_ge(s_hn, s - 1)
                    for g in range(2):
                        turn(s, NEW + g, [(Q, normed[:, k * P:(k + 1) * P]) for k in range(4 * g, 4 * g + 4)])
                if has_a:
                    pe.wait_ge(s_evac[0], evacuated(s, KD))
                    pe.wait_ge(s_evac[1], evacuated(s, KD + 1))
                    if has_d:
                        pe.wait_ge(s_acc, s - 2)
                for k in range(KD):
                    if has_a:
                        mm = nc.tensor.matmul(score_ps, qT[:, k, :], kT[:, k, :], start=(k == 0), stop=(k == KD - 1))
                        if k == KD - 1:
                            mm.then_inc(s_scores, 1)
                    if has_c and k == 2:
                        pe.wait_ge(s_evac[0], evacuated(s, NEW))
                        pe.wait_ge(s_evac[1], evacuated(s, NEW + 1))
                        pe.wait_ge(s_params, 64)
                        for j in range(KD):
                            mm = nc.tensor.matmul(logit_ps, hnT[:, j, :], wg[:, j, :], start=(j == 0),
                                                  stop=(j == KD - 1))
                        mm.then_inc(s_logit_ps, 1)

            stage1(pe, step)
            pe.wait_ge(s_sum, B)
            pe.wait_ge(s_acc, B)
            nc.tensor.matmul(count_ps, ones[:, :], chosen_sum[:, :], start=True, stop=True).then_inc(s_count, 1)

            def turn_rows(t):
                for k in range(KD):
                    mm = nc.tensor.transpose(xT_ps[:, k * P:(k + 1) * P], xg[t][:, k * P:(k + 1) * P], ident[:, :])
                return mm

            def turn_tile(e, t):
                pe.wait_ge(s_gath[t], 16 * e + 16)
                turn_rows(t).then_inc(s_xT[t], 1)

            def multiply(t, p, k, into):
                products = ((xh[t], wh[p]), (xh[t], wl[p]), (xl[t], wh[p]))
                for c, (rows, weights) in enumerate(products):
                    for n in range(2):
                        mm = nc.tensor.matmul(into[:, n * HB:(n + 1) * HB], rows[:, k, :],
                                              weights[:, k, n * HB:(n + 1) * HB],
                                              start=(k == 0 and c == 0), stop=(k == KD - 1 and c == 2))
                return mm

            def expert(e, p, last):
                over = pe.value_load(tile_table[0:1, 0, bass.ds(e, 1)], min_val=0, max_val=OVER)
                over_before = pe.value_load(tile_table[0:1, 1, bass.ds(e, 1)], min_val=0, max_val=OVER * E)
                pe.wait_ge(s_xl[0], e + 1)
                after(pe, s_yev[0], e)
                for k in range(KD):
                    if isinstance(e, int) and e == 0:
                        pe.wait_ge(s_wl0, k + 1)
                    else:
                        pe.wait_ge(s_wl, KD * (e - 1) + k + 1)
                    mm = multiply(0, p, k, y_ps[0])
                    if k == KD // 2:
                        turn_tile(e, 1)
                mm.then_inc(s_mm0, 1)
                with pe.If(over > 0):
                    wait_apart(pe, s_xl[1], e + 1)
                    with pe.Fori(0, OVER) as j:
                        with pe.If(over > j):
                            n = over_before + j
                            pe.wait_ge(o_gath, 16 * n + 16)
                            turn_rows(0).then_inc(o_xT, 1)
                            pe.wait_ge(o_xl, n + 1)
                            pe.wait_ge(o_yev, n + 1)
                            for k in range(KD):
                                mm = multiply(0, p, k, over_ps)
                            mm.then_inc(o_mm, 1)
                pe.wait_ge(s_xl[1], e + 1)
                after(pe, s_yev[1], e)
                for k in range(KD):
                    multiply(1, p, k, y_ps[1]).then_inc(s_wfree, 1)
                    if k == KD // 2 and not last:
                        turn_tile(e + 1, 0)

            pe.wait_ge(s_table, 1)
            turn_tile(0, 0)
            stage3(pe, expert)

        @block.scalar
        def _(act):
            def normalise(b, column, done_sem):
                nc.scalar.activation(normed[:, :], of_batch(x_all, b), ACT.Identity, bias=shift[:, bass.ds(column, 1)],
                                     scale=inv_std[:, bass.ds(column, 1)]).then_inc(done_sem, 1)

            def split_high(k, dst):
                nc.scalar.activation(at_k(dst, k), at_k(raw, k), ACT.Copy).then_inc(s_wh, 1)

            def turned(s, g, dst, cols):
                act.wait_ge(s_turned, group(s, g) + 1)
                nc.scalar.activation(dst, group_bank(s, g)[:, 0:cols], ACT.Copy).then_inc(s_evac[0], 1)

            def parameters():
                act.wait_ge(s_params, 64)
                nc.scalar.activation(tgx[:, :], gx[:, :], ACT.Tanh).then_inc(s_tanh, 1)
                nc.scalar.activation(tgf[:, :], gf[:, :], ACT.Tanh).then_inc(s_tanh, 1)
                act.wait_ge(s_tanh, 2)
                nc.scalar.mul(tgf_half[:, :], tgf[:, :], 1.0 / TOP_K).then_inc(s_tgf, 1)

            def step(s, p):
                has_a, has_b, has_c, _ = parts(s)
                if has_a and not (isinstance(s, int) and s == 0):
                    for g in range(0, 4, 2):
                        turned(s, g, kT[:, g, :], KV)
                if has_a:
                    act.wait_ge(s_xln, 1 if isinstance(s, int) and s == 0 else 2)
                    if not isinstance(s, int) or s >= 3:
                        act.wait_ge(s_turned, group(s - 1, NEW + 1) + 1)
                        act.wait_ge(s_hnstore, 16 * (s - 2))
                    elif s > 0:
                        act.wait_ge(s_turned, group(s - 1, KD + 1) + 1)
                    normalise(s, s, s_qn)
                    for g in range(0 if isinstance(s, int) and s == 0 else 4, KD - 2, 2):
                        turned(s, g, kT[:, g, :], KV)
                if has_b:
                    act.wait_ge(s_pT, s)
                    rows = KV_T[LAST][1]
                    nc.scalar.activation(probsT_h[:, 0:LAST, :].rearrange("p a q -> p (a q)"),
                                         probsT_ps[:, 0:LAST * Q], ACT.Copy)
                    nc.scalar.activation(probsT_h[0:rows, LAST, :], probsT_ps[0:rows, LAST * Q:(LAST + 1) * Q],
                                         ACT.Copy).then_inc(s_pTh, 1)
                if has_a:
                    turned(s, KD - 2, kT[:, KD - 2, :], KV)
                    turned(s, KD, qT[:, 0:4, :].rearrange("p k q -> p (k q)"), 4 * Q)
                if has_c:
                    act.wait_ge(s_hln, s - 1)
                    if has_a:
                        act.wait_ge(s_turned, group(s, KD + 1) + 1)
                    else:
                        act.wait_ge(s_turned, group(s - 1, NEW + 1) + 1)
                        act.wait_ge(s_hnstore, 16 * (s - 2))
                    normalise(s - 2, B, s_hn)
                    turned(s, NEW, hnT[:, 0:4, :].rearrange("p k q -> p (k q)"), 4 * Q)
                if has_a:
                    after(act, s_att, s)
                    for a, (_, rows) in enumerate(KV_T):
                        nc.scalar.activation(ctx_h[0:rows, a, :], ctx_t[p][0:rows, a, :], ACT.Copy).then_inc(s_ch, 1)
                if isinstance(s, int) and s == 0:
                    parameters()
                if has_b:
                    act.wait_ge(s_raw0, 16 * KD)
                    split_high(s - 1, wh[0])
                if has_a:
                    act.wait_ge(s_negmax, s + 1)
                    after(act, s_coef, s)
                    nc.scalar.activation(probs[:, :], score_ps, ACT.Exp, bias=neg_max[:, :],
                                         accum_out=prob_sum[:, :]).then_inc(s_probs, 1)

            stage1(act, step)
            act.wait_ge(s_slot_token, 1)
            act.wait_ge(s_hstore, 16 * B)
            act.wait_ge(s_hnstore, 16 * B)

            def split_rows(t):
                return nc.scalar.activation(xh[t][:, :, :].rearrange("p k m -> p (k m)"), xT_ps[:, :], ACT.Copy)

            def split_tile(e, t):
                act.wait_ge(s_xT[t], e + 1)
                if t == 0:
                    after(act, s_mm0, e)
                else:
                    after(act, s_wfree, KD * e)
                split_rows(t).then_inc(s_xh[t], 1)

            def weights(e, p, ks):
                for k in ks:
                    if not (isinstance(e, int) and e == 1):
                        act.wait_ge(s_wfree, KD * (e - 2) + k + 1)
                    act.wait_ge(s_raw[k], 16 * e)
                    split_high(k, wh[p])

            def expert(e, p, last):
                over = act.value_load(tile_table[0:1, 0, bass.ds(e, 1)], min_val=0, max_val=OVER)
                over_before = act.value_load(tile_table[0:1, 1, bass.ds(e, 1)], min_val=0, max_val=OVER * E)
                if not last:
                    weights(e + 1, 1 - p, range(0, 3))
                split_tile(e, 1)
                if not last:
                    weights(e + 1, 1 - p, range(3, 6))
                with act.If(over > 0):
                    with act.Fori(0, OVER) as j:
                        with act.If(over > j):
                            act.wait_ge(o_xT, over_before + j + 1)
                            split_rows(0).then_inc(o_xh, 1)
                    act.nop()
                if not last:
                    weights(e + 1, 1 - p, range(6, KD))
                    split_tile(e + 1, 0)

            act.wait_ge(s_table, 1)
            split_tile(0, 0)
            stage3(act, expert)

        @block.vector
        def _(dve):
            def measure(batches, call):
                for c, b in enumerate(batches):
                    rows = of_batch(x_all, b)
                    for half in range(2):
                        last = nc.vector.bn_stats(stats[:, c, half, :], rows[:, half * 512:(half + 1) * 512])
                last.then_inc(s_norm, 1)
                wait_apart(dve, s_norm, NORM_STEPS * call + 1)

            def norm_and_choose(call, n=0, at=0, ready=None, chosen_batch=None):
                made = [1 if n else 0]
                cols = slice(0, n)
                choice = chosen_batch is not None

                def link(last, alone=False):
                    made[0] += 1
                    last.then_inc(s_norm, 1)
                    if alone:
                        wait_apart(dve, s_norm, NORM_STEPS * call + made[0])
                    else:
                        dve.wait_ge(s_norm, NORM_STEPS * call + made[0])

                if choice:
                    dve.wait_ge(s_logit_ps, chosen_batch + 1)
                    last = nc.vector.tensor_tensor(logit[:, :], logit_ps, bg[0:Q, :], ALU.add)
                    other = logit[:, :].unsqueeze(1).to_broadcast([Q, E, E])
                    own = logit[:, :].unsqueeze(2).to_broadcast([Q, E, E])
                for c in range(n):
                    last = nc.vector.bn_aggr(mean_var[:, c, :], stats[:, c, :, :])
                link(last)
                if choice:
                    nc.vector.tensor_tensor(above[:, :, :], other, own, ALU.is_gt)
                    last = nc.vector.tensor_tensor(tied[:, :, :], other, own, ALU.is_equal)
                if n:
                    last = nc.vector.tensor_scalar(var_eps[:, cols], mean_var[:, cols, 1], EPS, None, ALU.add)
                link(last)
                if choice:
                    last = nc.vector.tensor_tensor(tied[:, :, :], tied[:, :, :], lower_e[:, :, :], ALU.mult)
                if n:
                    nc.vector.tensor_scalar(neg_half[:, cols], var_eps[:, cols], -0.5, None, ALU.mult)
                    last = nc.vector.tensor_scalar(half_bits[:, cols], var_eps[:, cols].bitcast(I32), 1, -1,
                                                   ALU.logical_shift_right, ALU.bitwise_xor)
                link(last, True)
                if n:
                    last = nc.vector.tensor_tensor(guess[0][:, cols].bitcast(I32), half_bits[:, cols],
                                                   seed_bits[:, cols], ALU.add)
                if choice:
                    last = nc.vector.tensor_tensor(above[:, :, :], above[:, :, :], tied[:, :, :], ALU.add)
                link(last)
                if choice:
                    last = nc.vector.tensor_reduce(place[:, :], above[:, :, :], AX.X, ALU.add)
                    if not n:
                        link(last)
                for j in range(NEWTON if n else 0):
                    r0 = guess[j][:, cols]
                    r1 = guess[j + 1][:, cols] if j + 1 < NEWTON else inv_std[:, at:at + n]
                    link(nc.vector.tensor_tensor(guess_sq[:, cols], r0, r0, ALU.mult))
                    link(nc.vector.tensor_tensor(guess_sq[:, cols], guess_sq[:, cols], neg_half[:, cols], ALU.mult))
                    link(nc.vector.scalar_tensor_tensor(out=r1, in0=guess_sq[:, cols], scalar=1.5, in1=r0,
                                                        op0=ALU.add, op1=ALU.mult))
                if n:
                    assert made[0] == NORM_STEPS
                    nc.vector.scalar_tensor_tensor(out=shift[:, at:at + n], in0=mean_var[:, cols, 0], scalar=-1.0,
                                                   in1=inv_std[:, at:at + n], op0=ALU.mult, op1=ALU.mult
                                                   ).then_inc(ready, 1)
                if choice:
                    nc.vector.tensor_scalar(chosen[:, :], place[:, :], float(TOP_K), None, ALU.is_lt).then_inc(s_chosen, 1)
                    nc.vector.tensor_tensor(onehot[:, :, :], place[:, :].unsqueeze(1).to_broadcast([Q, TOP_K, E]),
                                            choice_no[:, :, :], ALU.is_equal).then_inc(s_chosen_own, 1)

            def locate(b):
                base = SLOT_STEPS * b
                made = [0]

                def link(ins):
                    made[0] += 1
                    ins.then_inc(s_slot, 1)
                    dve.wait_ge(s_slot, base + made[0])

                dve.wait_ge(s_rank, b + 1)
                link(nc.vector.tensor_tensor(slot_of[:, :], rank_ps, expert_base[:, :], ALU.add))
                dve.wait_ge(s_chosen_own, b + 1)
                link(nc.vector.tensor_tensor(picked[:, :, :], slot_of[:, :].unsqueeze(1).to_broadcast([Q, TOP_K, E]),
                                             onehot[:, :, :], ALU.mult))
                with nc.allow_low_precision(reason="whole numbers below 2**13"):
                    link(nc.vector.tensor_reduce(slot_i[:, :], picked[:, :, :], AX.X, ALU.add))
                nc.vector.tensor_scalar(slot_col_i[:, :], slot_i[:, :], 7, None, ALU.logical_shift_right)
                link(nc.vector.tensor_scalar(slot_row_i[:, :], slot_i[:, :], P - 1, None, ALU.bitwise_and))
                nc.vector.tensor_copy(slot_col[:, :], slot_col_i[:, :])
                link(nc.vector.tensor_copy(slot_row[:, :], slot_row_i[:, :]))
                assert made[0] == SLOT_STEPS
                for c in range(TOP_K):
                    nc.vector.tensor_scalar(at_row[:, c, :], iota_slot[:, :], slot_row[:, c:c + 1], None, ALU.is_equal)
                    last = nc.vector.tensor_scalar(tok_col[:, c, :], iota_col[:, :], slot_col[:, c:c + 1],
                                                   tok_far[:, bass.ds(b, 1)], ALU.is_equal, ALU.mult)
                last.then_inc(s_tok_col, 1)
                nc.vector.tensor_tensor(chosen_sum[:, :], chosen_sum[:, :], chosen[:, :], ALU.add).then_inc(s_sum, 1)

            def add_slots(b):
                dve.wait_ge(s_slots_ps, b + 1)
                after(dve, s_acc, b)
                nc.vector.tensor_tensor(slot_acc[:, :], slot_acc[:, :], slot_ps, ALU.add).then_inc(s_acc, 1)

            def turned(s, g, dst, cols):
                dve.wait_ge(s_turned, group(s, g) + 1)
                nc.vector.tensor_copy(dst, group_bank(s, g)[:, 0:cols]).then_inc(s_evac[1], 1)

            dve.wait_ge(s_const, 1)
            dve.wait_ge(s_x0, 16)
            measure([0], 0)
            norm_and_choose(0, 1, 0, s_xln)

            def step(s, p):
                has_a, has_b, has_c, has_d = parts(s)
                if has_a:
                    for g in range(1, KD - 2, 2):
                        turned(s, g, kT[:, g, :], KV)
                if has_b:
                    dve.wait_ge(s_pTh, s)
                    rows = KV_T[LAST][1]
                    nc.vector.tensor_tensor(probsT_l[:, 0:LAST, :].rearrange("p a q -> p (a q)"), probsT_ps[:, 0:LAST * Q],
                                            probsT_h[:, 0:LAST, :].rearrange("p a q -> p (a q)"), ALU.subtract)
                    nc.vector.tensor_tensor(probsT_l[0:rows, LAST, :], probsT_ps[0:rows, LAST * Q:(LAST + 1) * Q],
                                            probsT_h[0:rows, LAST, :], ALU.subtract).then_inc(s_pTl, 1)
                if has_a:
                    turned(s, KD - 1, kT[:, KD - 1, :], KV)
                    turned(s, KD + 1, qT[:, 4:8, :].rearrange("p k q -> p (k q)"), 4 * Q)
                if has_b:
                    dve.wait_ge(s_tanh, 2)
                    dve.wait_ge(s_probs, s)
                    nc.vector.reciprocal(inv_sum[:, :], prob_sum[:, :]).then_inc(s_inv, 1)
                    dve.wait_ge(s_inv, s)
                    nc.vector.tensor_tensor(coef[:, :], inv_sum[:, :], tgx[0:Q, :], ALU.mult).then_inc(s_coef, 1)
                if has_d:
                    locate(s - 3)
                    add_slots(s - 3)
                if has_c:
                    turned(s, NEW + 1, hnT[:, 4:8, :].rearrange("p k q -> p (k q)"), 4 * Q)
                if has_b:
                    dve.wait_ge(s_coef, s)
                    dve.wait_ge(s_att, s)
                    rows = of_batch(x_all, s - 1)
                    nc.vector.scalar_tensor_tensor(out=rows, in0=att_ps, scalar=coef[:, 0:1], in1=rows,
                                                   op0=ALU.mult, op1=ALU.add).then_inc(s_h, 1)
                if isinstance(s, int) and s == 0:
                    dve.wait_ge(s_x, 16)
                    measure(range(1, B), 1)
                    norm_and_choose(1, B - 1, 1, s_xln)
                if has_b:
                    wait_apart(dve, s_h, s)
                    measure([s - 1], s + 1)
                    if has_c:
                        dve.wait_ge(s_hn, s - 1)
                    norm_and_choose(s + 1, 1, B, s_hln, s - 2 if has_c else None)
                elif has_c:
                    norm_and_choose(s + 1, chosen_batch=s - 2)
                if has_a:
                    dve.wait_ge(s_scores, s + 1)
                    after(dve, s_probs, s)
                    nc.vector.tensor_reduce(neg_max[:, :], score_ps, AX.X, ALU.max, negate=True).then_inc(s_negmax, 1)

            def split_low(e, k, p):
                dve.wait_ge(s_wh, KD * (e + 1) + k + 1)
                nc.vector.tensor_tensor(at_k(wl[p], k), at_k(raw, k), at_k(wh[p], k), ALU.subtract).then_inc(s_wl, 1)

            stage1(dve, step)

            made = [0]

            def link(ins):
                made[0] += 1
                ins.then_inc(s_last, 1)
                dve.wait_ge(s_last, made[0])

            dve.wait_ge(s_acc, B)
            link(nc.vector.tensor_scalar(used[:, :], slot_acc[:, :], 0.0, used_shift[:, 0:1], ALU.is_lt, ALU.mult))
            nc.vector.scalar_tensor_tensor(out=slot_token[:, :], in0=slot_acc[:, :], scalar=spare_row[:, 0:1],
                                           in1=used[:, :], op0=ALU.add, op1=ALU.add).then_inc(s_slot_token, 1)
            dve.wait_ge(s_count, 1)
            link(nc.vector.tensor_scalar(over_f[:, :], count_ps[0:1, :], float(-STATIC_TILES * P + P - 1), 0.0,
                                         ALU.add, ALU.max))
            link(nc.vector.tensor_copy(over_i[:, :], over_f[:, :]))
            link(nc.vector.tensor_scalar(tile_table[:, 0, :], over_i[:, :], 7, None, ALU.logical_shift_right))
            link(nc.vector.tensor_copy(over_e[:, :], tile_table[:, 0, :]))
            link(nc.vector.tensor_tensor(over_m[:, :, :], lower_e[0:1, :, :],
                                         over_e[:, :].unsqueeze(1).to_broadcast([1, E, E]), ALU.mult))
            link(nc.vector.tensor_reduce(over_b[:, :], over_m[:, :, :], AX.X, ALU.add))
            nc.vector.tensor_copy(tile_table[:, 1, :], over_b[:, :]).then_inc(s_table, 1)
            dve.wait_ge(s_hstore, 16 * B)
            dve.wait_ge(s_hnstore, 16 * B)

            dve.wait_ge(s_tgf, 1)
            dve.nop().then_inc(o_yev, 1)

            def split_rows(t):
                return nc.vector.tensor_tensor(xl[t][:, :, :].rearrange("p k m -> p (k m)"), xT_ps[:, :],
                                               xh[t][:, :, :].rearrange("p k m -> p (k m)"), ALU.subtract)

            def split_tile(e, t):
                dve.wait_ge(s_xh[t], e + 1)
                split_rows(t).then_inc(s_xl[t], 1)

            def weights(e, p, ks):
                for k in ks:
                    split_low(e - 1, k, p)

            def finish(banks, dst, evacuated_sem, n, ready):
                nc.vector.tensor_tensor(dst[:, :], banks[:, :], bias[:, :], ALU.add).then_inc(evacuated_sem, 1)
                dve.wait_ge(evacuated_sem, n)
                nc.vector.tensor_scalar(dst[:, :], dst[:, :], 0.0, tgf_half[:, 0:1], ALU.max, ALU.mult
                                        ).then_inc(ready, 1)

            def evacuate(e, t):
                if t == 0:
                    dve.wait_ge(s_mm0, e + 1)
                else:
                    dve.wait_ge(s_wfree, KD * e + KD)
                dve.wait_ge(s_bias, 16 * e + 16)
                if not (isinstance(e, int) and e == 0):
                    dve.wait_ge(s_added, 16 * (2 * e + t - 1))
                finish(y_ps[t], y[t], s_yev[t], e + 1, s_y)

            def expert(e, p, last):
                over = dve.value_load(tile_table[0:1, 0, bass.ds(e, 1)], min_val=0, max_val=OVER)
                over_before = dve.value_load(tile_table[0:1, 1, bass.ds(e, 1)], min_val=0, max_val=OVER * E)
                if not last:
                    weights(e + 1, 1 - p, range(0, 3))
                split_tile(e, 1)
                if not last:
                    weights(e + 1, 1 - p, range(3, 6))
                evacuate(e, 0)
                with dve.If(over > 0):
                    with dve.Fori(0, OVER) as j:
                        with dve.If(over > j):
                            n = over_before + j
                            dve.wait_ge(o_xh, n + 1)
                            split_rows(0).then_inc(o_xl, 1)
                            dve.wait_ge(o_mm, n + 1)
                            dve.wait_ge(o_free, n + 1)
                            finish(over_ps, y_over, o_yev, n + 2, o_y)
                    dve.nop()
                if not last:
                    weights(e + 1, 1 - p, range(6, KD))
                    split_tile(e + 1, 0)
                evacuate(e, 1)

            split_tile(0, 0)
            stage3(dve, expert)

        @block.gpsimd
        def _(pool):
            made = [0]

            def link(ins):
                made[0] += 1
                ins.then_inc(s_const0, 1)
                return made[0]

            g = nc.gpsimd
            link(g.memset(ident[:, :], 0.0))
            link(g.memset(before[:, :], 1.0))
            link(g.memset(lower_e[:, :, :], 1.0))
            link(g.memset(raw[:, KD - 1, :], 0.0))
            link(g.iota(seed_bits[:, :], [[0, B]], base=SEED_BITS, channel_multiplier=0))
            link(g.memset(ones[:, :], 1.0))
            link(g.memset(chosen_sum[:, :], 0.0))
            link(g.memset(slot_acc[:, :], 0.0))
            link(g.iota(choice_no[:, :, :], [[1, TOP_K], [0, E]], base=0, channel_multiplier=0,
                        allow_small_or_imprecise_dtypes=True))
            link(g.iota(iota_slot[:, :], [[1, P]], base=0, channel_multiplier=0, allow_small_or_imprecise_dtypes=True))
            link(g.iota(iota_col[:, :], [[1, COLS]], base=0, channel_multiplier=0, allow_small_or_imprecise_dtypes=True))
            link(g.iota(expert_base[:, :], [[MAX_TILES * P, E]], base=0, channel_multiplier=0,
                        allow_small_or_imprecise_dtypes=True))
            link(g.iota(tok_far[:, :], [[Q, B]], base=-FAR, channel_multiplier=1, allow_small_or_imprecise_dtypes=True))
            link(g.iota(spare_row[:, :], [[0, 1]], base=N_TOK, channel_multiplier=1, allow_small_or_imprecise_dtypes=True))
            link(g.iota(used_shift[:, :], [[0, 1]], base=FAR - N_TOK, channel_multiplier=-1,
                        allow_small_or_imprecise_dtypes=True))
            pool.wait_ge(s_const0, made[0])
            link(g.affine_select(out=ident[:, :], in_=ident[:, :], compare_op=ALU.not_equal, fill=1.0, base=0,
                                 pattern=[[-1, P]], channel_multiplier=1))
            link(g.affine_select(out=before[:, :], in_=before[:, :], compare_op=ALU.is_gt, fill=0.0, base=0,
                                 pattern=[[1, Q]], channel_multiplier=-1))
            link(g.affine_select(out=lower_e[:, :, :], in_=lower_e[:, :, :], compare_op=ALU.is_gt, fill=0.0, base=0,
                                 pattern=[[1, E], [-1, E]], channel_multiplier=0))
            pool.wait_ge(s_const0, made[0])
            pool.nop().then_inc(s_const, 1)
            for rows in (out, hn_rows):
                g.dma_start(rows[N_TOK:N_TOK + P, :], raw[:, KD - 1, :]).then_inc(s_zero, 16)

            def step(s, p):
                has_a, has_b, has_c, _ = parts(s)
                if has_c:
                    wait_apart(pool, s_hn, s - 1)
                    g.dma_start(hn_rows[bass.ds((s - 2) * Q, Q), :], normed[:, :]).then_inc(s_hnstore, 16)
                if has_b:
                    wait_apart(pool, s_h, s)
                    g.dma_start(out[bass.ds((s - 1) * Q, Q), :], of_batch(x_all, s - 1)).then_inc(s_hstore, 16)
                if has_a:
                    for a, (_, rows) in enumerate(KV_T):
                        pool.wait_ge(s_ch, 3 * s + a + 1)
                        last = g.tensor_tensor(ctx_l[0:rows, a, :], ctx_t[p][0:rows, a, :], ctx_h[0:rows, a, :],
                                               ALU.subtract)
                    last.then_inc(s_cl, 1)
                if has_b:
                    pool.wait_ge(s_wh, s)
                    g.tensor_tensor(at_k(wl[0], s - 1), at_k(raw, s - 1), at_k(wh[0], s - 1),
                                    ALU.subtract).then_inc(s_wl0, 1)

            stage1(pool, step)

            pool.wait_ge(s_slot_token, 1)
            pool.wait_ge(s_zero, 32)
            pool.wait_ge(s_hstore, 16 * B)
            pool.wait_ge(s_hnstore, 16 * B)

            def gather(dst, idx, done_sem):
                g.indirect_dma_start(dst[:, :], None, hn_rows, bass.IndirectOffsetOnAxis(idx, 0)).then_inc(done_sem, 16)

            def gather_tile(e, t, p):
                idx = idx_now[:, 2 * p + t:2 * p + t + 1]
                if not (isinstance(e, int) and e == 0):
                    pool.wait_ge(s_xT[t], e)
                if not (isinstance(e, int) and e < 2):
                    pool.wait_ge(s_added, 32 * (e - 2) + 16 * t + 16)
                g.tensor_copy(idx, slot_token[:, bass.ds(e * MAX_TILES + t, 1)]).then_inc(s_idx, 1)
                wait_apart(pool, s_idx, 2 * e + t + 1)
                gather(xg[t], idx, s_gath[t])

            def add_rows(rows, idx, added):
                g.indirect_dma_start(out, bass.IndirectOffsetOnAxis(idx, 0), rows[:, :], None,
                                     compute_op=ALU.add).then_inc(added, 16)

            def add_tile(e, t, p):
                pool.wait_ge(s_y, 2 * e + t + 1)
                if not (isinstance(e, int) and e == 0 and t == 0):
                    wait_apart(pool, s_added, 16 * (2 * e + t))
                add_rows(y[t], idx_now[:, 2 * p + t:2 * p + t + 1], s_added)

            def expert(e, p, last):
                over = pool.value_load(tile_table[0:1, 0, bass.ds(e, 1)], min_val=0, max_val=OVER)
                over_before = pool.value_load(tile_table[0:1, 1, bass.ds(e, 1)], min_val=0, max_val=OVER * E)
                with pool.If(over > 0):
                    pool.wait_ge(s_xT[0], e + 1)
                    wait_apart(pool, s_added, 32 * e)
                    idx = idx_now[:, 2 * STATIC_TILES:2 * STATIC_TILES + 1]
                    with pool.Fori(0, OVER) as j:
                        with pool.If(over > j):
                            n = over_before + j
                            g.tensor_copy(idx, slot_token[:, bass.ds(e * MAX_TILES + STATIC_TILES + j, 1)]).then_inc(o_idx, 1)
                            wait_apart(pool, o_idx, n + 1)
                            gather(xg[0], idx, o_gath)
                            wait_apart(pool, o_y, n + 1)
                            add_rows(y_over, idx, o_added)
                            pool.wait_ge(o_added, 16 * n + 16)
                            pool.nop().then_inc(o_free, 1)
                    pool.nop()
                if not last:
                    gather_tile(e + 1, 0, 1 - p)
                    gather_tile(e + 1, 1, 1 - p)
                add_tile(e, 0, p)
                add_tile(e, 1, p)

            gather_tile(0, 0, 0)
            gather_tile(0, 1, 0)
            pool.wait_ge(s_table, 1)
            pool.nop().then_inc(o_free, 1)
            stage3(pool, expert)
            pool.wait_ge(s_added, 16 * 2 * E)


NEWTON = 3
SEED_BITS = 0x5F3759DF + 1
NORM_STEPS = 5 + 3 * NEWTON

SLOT_STEPS = 5

_INS = ["x", "ctx_4096", "g_xattn", "g_ffn", "L0_ffn_W_gate", "L0_ffn_b_gate", "L0_ffn_W_e", "L0_ffn_b_e"]


def kernel(**inputs):
    import numpy as np
    import concourse.bacc as bacc
    from concourse.bass_utils import run_bass_kernel_spmd

    nc = bacc.Bacc("TRN2", target_bir_lowering=False, num_devices=1)
    arrays, args = {}, []
    for name in _INS:
        a = np.ascontiguousarray(inputs[name])
        arrays[f"in_{name}"] = a
        args.append(nc.dram_tensor(f"in_{name}", a.shape, mybir.dt.from_np(a.dtype), kind="ExternalInput").ap())
    b, q, d = inputs["x"].shape
    out = nc.dram_tensor("out_rows", [b * q + P, d], F32, kind="ExternalOutput").ap()
    gated_block(nc, *args, out)
    r = run_bass_kernel_spmd(nc, [arrays], core_ids=[0])
    return r.results[0]["out_rows"][:b * q].reshape(b, q, d)
```

```python
from contextlib import ExitStack

import concourse.bass as bass
from concourse import mybir

F32 = mybir.dt.float32
F32R = mybir.dt.float32r
F16 = mybir.dt.float16
I32 = mybir.dt.int32
ALU = mybir.AluOpType
ACT = mybir.ActivationFunctionType
AX = mybir.AxisListType

P = 128
EPS = 1e-5
TOP_K = 2
STATIC_TILES = 2
FAR = 1000


def gated_block(nc, x, ctx_kv, g_xattn, g_ffn, w_gate, b_gate, w_e, b_e, out):
    B, Q, D = x.shape
    KV = ctx_kv.shape[1]
    E = w_gate.shape[1]
    H = w_e.shape[2]
    KD = D // P
    HB = H // 2
    N_TOK = B * Q
    KV_T = [(a, min(P, KV - a)) for a in range(0, KV, P)]
    LAST = len(KV_T) - 1
    MAX_TILES = -(-N_TOK // P)
    OVER = MAX_TILES - STATIC_TILES
    COLS = E * MAX_TILES
    assert out.shape[0] == N_TOK + P and H == D and E == KD and B % 2 == 0 and E % 2 == 0
    assert N_TOK < FAR

    es = ExitStack()
    with es:
        def sb(name, shape, dt=F32, stack=es):
            return stack.enter_context(nc.sbuf_tensor(name, shape, dt))

        def sem(name):
            return es.enter_context(nc.semaphore(name))

        hn_rows = nc.dram_tensor("hn_rows", [N_TOK + P, D], F32, kind="Internal").ap()

        ident = sb("ident", [P, P])
        before = sb("before", [Q, Q], F16)
        ones = sb("ones", [Q, Q], F16)
        iota_slot = sb("iota_slot", [Q, P], F16)
        iota_col = sb("iota_col", [Q, COLS], F16)
        expert_base = sb("expert_base", [Q, E])
        choice_no = sb("choice_no", [Q, TOP_K, E])
        tok_far = sb("tok_far", [Q, B])
        spare_row = sb("spare_row", [P, 1])
        used_shift = sb("used_shift", [P, 1])
        seed_bits = sb("seed_bits", [Q, B + 1], I32)
        lower_e = sb("lower_e", [Q, E, E])
        wg = sb("wg", [P, KD, E])
        bg = sb("bg", [P, E])
        gx = sb("gx", [P, 1])
        gf = sb("gf", [P, 1])
        tgx = sb("tgx", [P, 1])
        tgf = sb("tgf", [P, 1])
        tgf_half = sb("tgf_half", [P, 1])
        tile_table = sb("tile_table", [1, 2, E], I32)
        slot_token = sb("slot_token", [P, COLS], I32)
        early_flag = sb("early_flag", [1, 1], I32)
        early_token = sb("early_token", [P, 1], I32)
        idx_now = sb("idx_now", [P, 2 * STATIC_TILES + 1], I32)

        raw = sb("raw", [P, KD, H])
        wh = [sb("wh0", [P, KD, H], F32R), None]
        wl = [sb("wl0", [P, KD, H], F32R), None]

        att = ExitStack()
        ctx_t = [sb(f"ctx{p}", [P, len(KV_T), D], stack=att) for p in range(2)]
        ctx_h = sb("ctx_h", [P, len(KV_T), D], F32R, stack=att)
        ctx_l = sb("ctx_l", [P, len(KV_T), D], F32R, stack=att)
        kT = sb("kT", [P, KD, KV], stack=att)
        x_all = sb("x_all", [Q, B, D], stack=att)
        normed = sb("normed", [Q, D], stack=att)
        qT = sb("qT", [P, KD, Q], stack=att)
        probs = sb("probs", [Q, KV], stack=att)
        probsT_h = sb("probsT_h", [P, len(KV_T), Q], F32R, stack=att)
        probsT_l = sb("probsT_l", [P, len(KV_T), Q], F32R, stack=att)
        hnT = sb("hnT", [P, KD, Q], stack=att)
        stats = sb("stats", [Q, B + 1, 2, 6], stack=att)
        mean_var = sb("mean_var", [Q, B + 1, 2], stack=att)
        var_eps = sb("var_eps", [Q, B + 1], stack=att)
        neg_half = sb("neg_half", [Q, B + 1], stack=att)
        half_bits = sb("half_bits", [Q, B + 1], I32, stack=att)
        guess = [sb(f"guess{j}", [Q, B + 1], stack=att) for j in range(NEWTON)]
        guess_sq = sb("guess_sq", [Q, B + 1], stack=att)
        inv_std = sb("inv_std", [Q, B + 1], stack=att)
        shift = sb("shift", [Q, B + 1], stack=att)
        neg_max = sb("neg_max", [Q, 1], stack=att)
        prob_sum = sb("prob_sum", [Q, 1], stack=att)
        inv_sum = sb("inv_sum", [Q, 1], stack=att)
        coef = sb("coef", [Q, 1], stack=att)
        logit = sb("logit", [Q, E], stack=att)
        above = sb("above", [Q, E, E], stack=att)
        tied = sb("tied", [Q, E, E], stack=att)
        place = sb("place", [Q, E], stack=att)
        onehot = sb("onehot", [Q, TOP_K, E], stack=att)
        chosen = sb("chosen", [Q, E], F16, stack=att)
        chosen_sum = sb("chosen_sum", [Q, E], F16, stack=att)
        slot_of = sb("slot_of", [Q, E], stack=att)
        picked = sb("picked", [Q, TOP_K, E], stack=att)
        slot_i = sb("slot_i", [Q, TOP_K], I32, stack=att)
        slot_col_i = sb("slot_col_i", [Q, TOP_K], I32, stack=att)
        slot_row_i = sb("slot_row_i", [Q, TOP_K], I32, stack=att)
        slot_col = sb("slot_col", [Q, TOP_K], stack=att)
        slot_row = sb("slot_row", [Q, TOP_K], stack=att)
        at_row = sb("at_row", [Q, TOP_K, P], F16, stack=att)
        tok_col = sb("tok_col", [Q, TOP_K, COLS], F16, stack=att)
        slot_acc = sb("slot_acc", [P, COLS], stack=att)
        used = sb("used", [P, COLS], stack=att)
        over_f = sb("over_f", [1, E], stack=att)
        over_i = sb("over_i", [1, E], I32, stack=att)
        over_e = sb("over_e", [1, E], stack=att)
        over_m = sb("over_m", [1, E, E], stack=att)
        over_b = sb("over_b", [1, E], stack=att)
        att.close()

        xg, xh, xl = [], [], []
        xg.append(sb("xg0", [P, D]))
        xh.append(sb("xh0", [P, KD, P], F32R))
        xl.append(sb("xl0", [P, KD, P], F32R))
        assert 3 * D <= len(KV_T) * D
        wh[1] = sb("wh1", [P, KD, H], F32R)
        wl[1] = sb("wl1", [P, KD, H], F32R)
        xg.append(sb("xg1", [P, D]))
        xh.append(sb("xh1", [P, KD, P], F32R))
        xl.append(sb("xl1", [P, KD, P], F32R))
        y = sb("y", [P, H])
        over_rows = sb("over_rows", [P, D])
        xh_over = sb("xh_over", [P, KD, P], F32R)
        xl_over = sb("xl_over", [P, KD, P], F32R)
        bias = sb("bias", [P, H])

        ps = [es.enter_context(nc.psum_tensor(f"ps{j}", [P, 2 * 512], F32)) for j in range(4)]
        turn_bank = [ps[j // 2][:, 512 * (j % 2):512 * (j % 2) + 512] for j in range(4)]
        score_ps = ps[2][0:Q, 0:KV]
        rank_ps = ps[2][0:Q, 368:368 + E]
        count_ps = ps[2][0:Q, 384:384 + E]
        probsT_ps = ps[2][:, 512:512 + len(KV_T) * Q]
        logit_ps = ps[2][0:Q, 840:840 + E]
        slot_ps = ps[2][:, 864:864 + COLS]
        att_ps = ps[3][0:Q, 0:D]
        xT_ps, over_ps = ps[0], ps[1]
        y_ps = (ps[3], ps[2])

        s_params = sem("params_loaded")
        s_const0 = sem("const_filled")
        s_const = sem("const_ready")
        s_tanh = sem("tanh_ready")
        s_tgf = sem("tgf_half_ready")
        s_zero = sem("spare_rows_zeroed")
        s_x0 = sem("x0_loaded")
        s_x_early = sem("x_early_loaded")
        s_x_late = sem("x_late_loaded")
        s_ctx0 = [sem(f"ctx0_loaded{half}") for half in range(2)]
        s_ctx = [sem(f"ctx_loaded{p}") for p in range(2)]
        s_raw_first = sem("raw_loaded_first")
        s_raw_rest = sem("raw_loaded_rest")
        s_raw = [sem(f"raw_loaded{k}") for k in range(KD)]
        s_turned = sem("turned")
        s_evac = [sem("evac_act"), sem("evac_dve")]
        s_norm = sem("norm_step")
        s_xln = sem("x_norm_ready")
        s_hln = sem("h_norm_ready")
        s_qn = sem("qn_ready")
        s_scores = sem("scores_ready")
        s_negmax = sem("neg_max_ready")
        s_probs = sem("probs_ready")
        s_inv = sem("inv_sum_ready")
        s_coef = sem("coef_ready")
        s_pT = sem("probs_turned")
        s_pTh = sem("probsT_high_ready")
        s_pTl = sem("probsT_low_ready")
        s_ch = sem("ctx_high_ready")
        s_cl = sem("ctx_low_ready")
        s_att = sem("attention_ready")
        s_h = sem("h_ready")
        s_hn = sem("hn_ready")
        s_logit_ps = sem("logits_multiplied")
        s_hstore = sem("h_stored")
        s_hnstore = sem("hn_stored")
        s_wh = sem("w_high_ready")
        s_wl = sem("w_low_ready")
        s_wl0 = sem("w_low_ready_first")
        s_wfree = sem("w_used")
        s_chosen = sem("chosen_ready")
        s_chosen_own = sem("onehot_ready")
        s_rank = sem("ranks_ready")
        s_sum = sem("chosen_summed")
        s_slot = sem("slot_step")
        s_tok_col = sem("tok_col_ready")
        s_slots_ps = sem("slots_ready")
        s_acc = sem("slots_added")
        s_count = sem("counts_ready")
        s_last = sem("table_step")
        s_table = sem("tile_table_ready")
        s_slot_token = sem("slot_token_ready")
        s_bias = sem("bias_loaded")
        s_early_count = sem("early_count_ready")
        s_early_step = sem("early_step")
        s_early = sem("early_flag_ready")
        s_idx = sem("idx_staged")
        s_gath = [sem(f"gathered{t}") for t in range(2)]
        s_xT = [sem(f"x_turned{t}") for t in range(2)]
        s_xh = [sem(f"x_high_ready{t}") for t in range(2)]
        s_xl = [sem(f"x_low_ready{t}") for t in range(2)]
        s_mm0 = sem("tile0_multiplied")
        s_yev = [sem(f"y_evacuated{t}") for t in range(2)]
        s_y = sem("y_ready")
        s_added = sem("y_added")
        o_idx = sem("over_idx_staged")
        o_gath = sem("over_gathered")
        o_xT = sem("over_x_turned")
        o_xh = sem("over_x_high_ready")
        o_xl = sem("over_x_low_ready")
        o_mm = sem("over_multiplied")
        o_yev = sem("over_y_evacuated")
        o_y = sem("over_y_ready")
        o_added = sem("over_y_added")

        def wait_apart(eng, semaphore, value):
            if not isinstance(value, int):
                value = eng.to_reg(value)
            eng.wait_ge(s_const, 1)
            eng.wait_ge(semaphore, value)

        def of_batch(tile, b):
            return tile[:, bass.ds(b, 1), :].rearrange("q a n -> q (a n)")

        def at_k(tile, k):
            return tile[:, bass.ds(k, 1), :].rearrange("p a n -> p (a n)")

        FIRST_K = 2

        x_early, x_late = range(1, B - 4), range(B - 4, B)

        EARLY = {B: range(0, 1), B + 1: range(1, 2), B + 2: range(2, 4), "after": range(4, KD)}

        def load_early(eng):
            eng.wait_ge(s_early, 1)
            return eng.value_load(early_flag[0:1, 0:1], min_val=0, max_val=1)

        def after(eng, semaphore, value):
            if not (isinstance(value, int) and value == 0):
                eng.wait_ge(semaphore, value)

        def stage1(eng, step):
            for s in range(3):
                step(s, s % 2)
            with eng.Fori(1, B // 2 - 1) as i:
                step(2 * i + 1, 1)
                step(2 * i + 2, 0)
            for s in range(B - 1, B + 3):
                step(s, s % 2)

        def parts(s):
            if not isinstance(s, int):
                return True, True, True, True
            return s < B, 1 <= s <= B, 2 <= s <= B + 1, s >= 3

        def stage3(eng, expert):
            expert(0, 0, False)
            expert(1, 1, False)
            with eng.Fori(1, E // 2 - 1) as i:
                expert(2 * i, 0, False)
                expert(2 * i + 1, 1, False)
            expert(E - 2, 0, False)
            expert(E - 1, 1, True)

        NEW = KD + 2
        GROUPS = NEW + 2

        def group(s, g):
            if not isinstance(s, int):
                return GROUPS * s - 4 + g
            before_s = sum(NEW * (c < B) + 2 * (2 <= c <= B + 1) for c in range(s))
            return before_s + (g if s < B else g - NEW)

        def group_bank(s, g):
            return turn_bank[(group(s, g) if isinstance(s, int) else g) % 4]

        def evacuated(s, g):
            if not isinstance(s, int):
                return GROUPS // 2 * s - 2 + g // 2 + 1
            return group(s, g) // 2 + 1

        block = es.enter_context(nc.Block())

        @block.sync
        def _(sp):
            def load_parameters():
                sp.dma_start(wg[:, :, :], w_gate.rearrange("(k p) e -> p k e", p=P)).then_inc(s_params, 16)
                sp.dma_start(bg[:, :], b_gate.partition_broadcast(P)).then_inc(s_params, 16)
                for g, t in ((g_xattn, gx), (g_ffn, gf)):
                    sp.dma_start(t[:, :], g.partition_broadcast(P)).then_inc(s_params, 16)

            def load_context(b, p):
                sp.dma_start(ctx_t[p][:, 0:LAST, :],
                             ctx_kv[b, 0:P * LAST, :].rearrange("(a p) d -> p a d", p=P)).then_inc(s_ctx[p], 16)
                first, rows = KV_T[LAST]
                sp.dma_start(ctx_t[p][0:rows, LAST, :], ctx_kv[b, first:KV, :]).then_inc(s_ctx[p], 16)

            def load_queries(batches, loaded):
                a, b = batches.start, batches.stop
                sp.dma_start(x_all[:, a:b, :], x[a:b, :, :].rearrange("b q d -> q b d")).then_inc(loaded, 16)

            def load_weights(e, k, loaded):
                sp.dma_start(raw[:, k, :], w_e[e, k * P:(k + 1) * P, :]).then_inc(loaded, 16)

            def load_bias(e):
                sp.dma_start(bias[:, :], b_e[e, :].partition_broadcast(P)).then_inc(s_bias, 16)

            sp.dma_start(x_all[:, 0, :], x[0, :, :]).then_inc(s_x0, 16)
            first, rows = KV_T[LAST]
            for half, cols in enumerate((slice(0, D // 2), slice(D // 2, D))):
                sp.dma_start(ctx_t[0][:, 0:LAST, cols], ctx_kv[0, 0:first, cols].rearrange("(a p) d -> p a d", p=P)
                             ).then_inc(s_ctx0[half], 16)
                sp.dma_start(ctx_t[0][0:rows, LAST, cols], ctx_kv[0, first:KV, cols]).then_inc(s_ctx0[half], 16)
            load_queries(x_early, s_x_early)
            load_context(1, 1)
            load_queries(x_late, s_x_late)
            load_parameters()
            for k in range(FIRST_K):
                load_weights(0, k, s_raw_first)

            def step(s, p):
                if isinstance(s, int) and (s == 0 or s > B - 2):
                    return
                sp.wait_ge(s_cl, s)
                sp.wait_ge(s_turned, group(s - 1, KD - 1) + 1)
                load_context(s + 1, 1 - p)
                if isinstance(s, int) and s == 1:
                    sp.wait_ge(s_zero, 32)
                    for k in range(FIRST_K, KD):
                        load_weights(0, k, s_raw_rest)

            stage1(sp, step)

            for k in range(KD):
                sp.wait_ge(s_wl0, k + 1)
                load_weights(1, k, s_raw[k])

            for t in range(2):
                sp.wait_ge(s_gath[t], 16)
            sp.wait_ge(s_table, 1)
            load_bias(0)

            def weights_of(e, p):
                for k in range(KD):
                    sp.wait_ge(s_wl, KD * (e - 1) + k + 1)
                    load_weights(e + 1, k, s_raw[k])
                sp.wait_ge(s_yev[1], e)
                load_bias(e)

            weights_of(1, 1)
            with sp.Fori(1, E // 2 - 1) as i:
                weights_of(2 * i, 0)
                weights_of(2 * i + 1, 1)
            weights_of(E - 2, 0)
            sp.wait_ge(s_yev[1], E - 1)
            load_bias(E - 1)

        @block.tensor
        def _(pe):
            pe.wait_ge(s_const, 1)
            early = []

            def turn_rows(rows):
                for k in range(KD):
                    mm = nc.tensor.transpose(xT_ps[:, k * P:(k + 1) * P], rows[:, k * P:(k + 1) * P], ident[:, :])
                return mm

            def turn_tile(e, t):
                pe.wait_ge(s_gath[t], 16 * e + 16)
                turn_rows(xg[t]).then_inc(s_xT[t], 1)

            def multiply(high, low, p, k, into, products=range(3)):
                for c in products:
                    rows, weights = ((high, wh[p]), (high, wl[p]), (low, wh[p]))[c]
                    for n in range(2):
                        mm = nc.tensor.matmul(into[:, n * HB:(n + 1) * HB], rows[:, k, :],
                                              weights[:, k, n * HB:(n + 1) * HB],
                                              start=(k == 0 and c == 0), stop=(k == KD - 1 and c == 2))
                return mm

            def multiply_high(t, ks):
                for k in ks:
                    pe.wait_ge(s_wl0, k + 1)
                    multiply(xh[t], xl[t], 0, k, y_ps[t], (0, 1))

            def multiply_low(t, ks):
                for k in ks:
                    mm = multiply(xh[t], xl[t], 0, k, y_ps[t], (2,))
                return mm

            def multiply_early(ks):
                with pe.If(early[0] > 0):
                    pe.wait_ge(s_xh[0], 1)
                    pe.wait_ge(s_h, B)
                    multiply_high(0, ks)

            def multiply_slots(s):
                pe.wait_ge(s_tok_col, s - 2)
                for c in range(TOP_K):
                    mm = nc.tensor.matmul(slot_ps, at_row[:, c, :], tok_col[:, c, :], start=(c == 0),
                                          stop=(c == TOP_K - 1))
                mm.then_inc(s_slots_ps, 1)

            def turn(s, g, blocks):
                bank = group_bank(s, g)
                n = group(s, g)
                if not isinstance(n, int) or n >= 4:
                    pe.wait_ge(s_evac[g % 2], evacuated(s, g) - 2)
                at = 0
                for rows, src in blocks:
                    mm = nc.tensor.transpose(bank[:, at:at + rows], src, ident[0:rows, 0:rows])
                    at += rows
                mm.then_inc(s_turned, 1)

            def step(s, p):
                has_a, has_b, has_c, has_d = parts(s)
                slots_first = isinstance(s, int) and s == B

                def turn_context(groups):
                    for g in groups:
                        turn(s, g, [(rows, ctx_t[p][0:rows, a, g * P:(g + 1) * P])
                                    for a, (_, rows) in enumerate(KV_T)])

                if has_a:
                    if isinstance(s, int) and s == 0:
                        pe.wait_ge(s_ctx0[0], 32)
                        turn_context(range(0, KD // 2))
                        pe.wait_ge(s_ctx0[1], 32)
                        turn_context(range(KD // 2, KD - 2))
                    else:
                        pe.wait_ge(s_ctx[p], 16 * (s + p))
                        turn_context(range(0, KD - 2))
                if has_b:
                    pe.wait_ge(s_probs, s)
                    if has_d:
                        pe.wait_ge(s_chosen, s - 2)
                    for a, (first, rows) in enumerate(KV_T):
                        mm = nc.tensor.transpose(probsT_ps[0:rows, a * Q:(a + 1) * Q],
                                                 probs[:, first:first + rows], ident[0:Q, 0:Q])
                    mm.then_inc(s_pT, 1)
                if has_d:
                    pe.wait_ge(s_chosen, s - 2)
                    if not isinstance(s, int) or s > 3:
                        pe.wait_ge(s_sum, s - 3)
                    nc.tensor.matmul(rank_ps, before[:, :], chosen[:, :], start=True, stop=False)
                    nc.tensor.matmul(rank_ps, ones[:, :], chosen_sum[:, :], start=False, stop=True).then_inc(s_rank, 1)
                if has_a:
                    turn_context(range(KD - 2, KD))
                    pe.wait_ge(s_qn, s + 1)
                    for g in range(2):
                        turn(s, KD + g, [(Q, normed[:, k * P:(k + 1) * P]) for k in range(4 * g, 4 * g + 4)])
                if has_b:
                    after(pe, s_h, s - 1)
                    pe.wait_ge(s_pTl, s)
                    pe.wait_ge(s_cl, s)
                    for n in range(2):
                        if slots_first and n == 1:
                            multiply_slots(s)
                            pe.wait_ge(s_sum, B - 2)
                            nc.tensor.matmul(count_ps, ones[:, :], chosen_sum[:, :], start=True, stop=True
                                             ).then_inc(s_early_count, 1)
                        cols = slice(n * 512, (n + 1) * 512)
                        for a, (_, rows) in enumerate(KV_T):
                            products = ((probsT_h, ctx_h), (probsT_h, ctx_l), (probsT_l, ctx_h))
                            for c, (weights, values) in enumerate(products):
                                mm = nc.tensor.matmul(att_ps[:, cols], weights[0:rows, a, :], values[0:rows, a, cols],
                                                      start=(a == 0 and c == 0), stop=(a == LAST and c == 2))
                    mm.then_inc(s_att, 1)
                if has_c:
                    pe.wait_ge(s_hn, s - 1)
                    for g in range(2):
                        turn(s, NEW + g, [(Q, normed[:, k * P:(k + 1) * P]) for k in range(4 * g, 4 * g + 4)])
                if isinstance(s, int) and s == B + 2:
                    multiply_early(EARLY[s])
                if has_d and not slots_first:
                    multiply_slots(s)
                if has_a:
                    pe.wait_ge(s_evac[0], evacuated(s, KD))
                    pe.wait_ge(s_evac[1], evacuated(s, KD + 1))
                for k in range(KD):
                    if has_a:
                        mm = nc.tensor.matmul(score_ps, qT[:, k, :], kT[:, k, :], start=(k == 0), stop=(k == KD - 1))
                        if k == KD - 1:
                            mm.then_inc(s_scores, 1)
                    if has_c and k == 2:
                        pe.wait_ge(s_evac[0], evacuated(s, NEW))
                        pe.wait_ge(s_evac[1], evacuated(s, NEW + 1))
                        pe.wait_ge(s_params, 64)
                        if has_d:
                            pe.wait_ge(s_acc, s - 2)
                        for j in range(KD):
                            mm = nc.tensor.matmul(logit_ps, hnT[:, j, :], wg[:, j, :], start=(j == 0),
                                                  stop=(j == KD - 1))
                        mm.then_inc(s_logit_ps, 1)
                if isinstance(s, int) and s == B:
                    early.append(load_early(pe))
                    with pe.If(early[0] > 0):
                        turn_tile(0, 0)
                    multiply_early(EARLY[s])
                if isinstance(s, int) and s == B + 1:
                    multiply_early(EARLY[s])

            stage1(pe, step)
            pe.wait_ge(s_sum, B)
            pe.wait_ge(s_acc, B)
            nc.tensor.matmul(count_ps, ones[:, :], chosen_sum[:, :], start=True, stop=True).then_inc(s_count, 1)

            def expert(e, p, last):
                over = pe.value_load(tile_table[0:1, 0, bass.ds(e, 1)], min_val=0, max_val=OVER)
                over_before = pe.value_load(tile_table[0:1, 1, bass.ds(e, 1)], min_val=0, max_val=OVER * E)

                def turn_over(j):
                    pe.wait_ge(o_gath, 16 * (over_before + j) + 16)
                    turn_rows(over_rows).then_inc(o_xT, 1)

                def multiply_over(j):
                    n = over_before + j
                    pe.wait_ge(o_xl, n + 1)
                    pe.wait_ge(o_yev, n + 1)
                    for k in range(KD):
                        mm = multiply(xh_over, xl_over, p, k, over_ps)
                    mm.then_inc(o_mm, 1)

                first = isinstance(e, int) and e == 0
                if first:
                    with pe.If(over > 0):
                        wait_apart(pe, s_xl[1], 1)
                        turn_over(0)
                else:
                    pe.wait_ge(s_xl[0], e + 1)
                    pe.wait_ge(s_yev[0], e)
                    for k in range(KD):
                        if k == 1:
                            turn_tile(e, 1)
                        if k == 5:
                            with pe.If(over > 0):
                                wait_apart(pe, s_xl[1], e + 1)
                                turn_over(0)
                        pe.wait_ge(s_wl, KD * (e - 1) + k + 1)
                        mm = multiply(xh[0], xl[0], p, k, y_ps[0])
                    mm.then_inc(s_mm0, 1)
                with pe.If(over > 0):
                    multiply_over(0)
                    with pe.If(over > 1):
                        with pe.Fori(1, OVER) as j:
                            with pe.If(over > j):
                                turn_over(j)
                                multiply_over(j)
                        pe.nop()
                    pe.nop()
                if first:
                    pe.wait_ge(s_xh[1], 1)
                    multiply_high(1, range(KD))
                pe.wait_ge(s_xl[1], e + 1)
                after(pe, s_yev[1], e)
                for k in range(KD):
                    multiply(xh[1], xl[1], p, k, y_ps[1], (2,) if first else range(3)).then_inc(s_wfree, 1)
                    if k == (1 if first else KD // 2) and not last:
                        turn_tile(e + 1, 0)

            multiply_early(EARLY["after"])
            with pe.If(early[0] < 1):
                turn_tile(0, 0)
                pe.wait_ge(s_xh[0], 1)
                multiply_high(0, range(KD))
            pe.wait_ge(s_xl[0], 1)
            multiply_low(0, range(0, KD // 2))
            turn_tile(0, 1)
            multiply_low(0, range(KD // 2, KD)).then_inc(s_mm0, 1)
            pe.wait_ge(s_table, 1)
            stage3(pe, expert)

        @block.scalar
        def _(act):
            def normalise(b, column, done_sem):
                nc.scalar.activation(normed[:, :], of_batch(x_all, b), ACT.Identity, bias=shift[:, bass.ds(column, 1)],
                                     scale=inv_std[:, bass.ds(column, 1)]).then_inc(done_sem, 1)

            def split_high(k, dst):
                nc.scalar.activation(at_k(dst, k), at_k(raw, k), ACT.Copy).then_inc(s_wh, 1)

            def turned(s, g, dst, cols):
                act.wait_ge(s_turned, group(s, g) + 1)
                nc.scalar.activation(dst, group_bank(s, g)[:, 0:cols], ACT.Copy).then_inc(s_evac[0], 1)

            def split_rows(high):
                return nc.scalar.activation(high[:, :, :].rearrange("p k m -> p (k m)"), xT_ps[:, :], ACT.Copy)

            def split_tile(e, t):
                act.wait_ge(s_xT[t], e + 1)
                if t == 0:
                    after(act, s_mm0, e)
                else:
                    after(act, s_wfree, KD * e)
                split_rows(xh[t]).then_inc(s_xh[t], 1)

            early = []

            def parameters():
                act.wait_ge(s_params, 64)
                nc.scalar.activation(tgx[:, :], gx[:, :], ACT.Tanh).then_inc(s_tanh, 1)
                nc.scalar.activation(tgf[:, :], gf[:, :], ACT.Tanh).then_inc(s_tanh, 1)
                act.wait_ge(s_tanh, 2)
                nc.scalar.mul(tgf_half[:, :], tgf[:, :], 1.0 / TOP_K).then_inc(s_tgf, 1)

            def normalise_queries(b):
                act.wait_ge(s_xln, 1 if isinstance(b, int) and b == 0 else 2)
                if not isinstance(b, int) or b >= 3:
                    act.wait_ge(s_turned, group(b - 1, NEW + 1) + 1)
                    act.wait_ge(s_hnstore, 16 * (b - 2))
                elif b > 0:
                    act.wait_ge(s_turned, group(b - 1, KD + 1) + 1)
                normalise(b, b, s_qn)

            def step(s, p):
                has_a, has_b, has_c, _ = parts(s)
                if has_a:
                    turned(s, 2, kT[:, 2, :], KV)
                if isinstance(s, int) and s < 2:
                    normalise_queries(s)
                if has_a:
                    for g in range(4, KD - 2, 2):
                        turned(s, g, kT[:, g, :], KV)
                if has_b:
                    act.wait_ge(s_pT, s)
                    rows = KV_T[LAST][1]
                    nc.scalar.activation(probsT_h[:, 0:LAST, :].rearrange("p a q -> p (a q)"),
                                         probsT_ps[:, 0:LAST * Q], ACT.Copy)
                    nc.scalar.activation(probsT_h[0:rows, LAST, :], probsT_ps[0:rows, LAST * Q:(LAST + 1) * Q],
                                         ACT.Copy).then_inc(s_pTh, 1)
                if has_a:
                    turned(s, KD - 2, kT[:, KD - 2, :], KV)
                    turned(s, KD, qT[:, 0:4, :].rearrange("p k q -> p (k q)"), 4 * Q)
                if isinstance(s, int) and s == 1:
                    parameters()
                if has_c:
                    act.wait_ge(s_hln, s - 1)
                    if has_a:
                        act.wait_ge(s_turned, group(s, KD + 1) + 1)
                    else:
                        act.wait_ge(s_turned, group(s - 1, NEW + 1) + 1)
                        act.wait_ge(s_hnstore, 16 * (s - 2))
                    normalise(s - 2, B, s_hn)
                    turned(s, NEW, hnT[:, 0:4, :].rearrange("p k q -> p (k q)"), 4 * Q)
                if has_a:
                    after(act, s_att, s)
                    for a, (_, rows) in enumerate(KV_T):
                        nc.scalar.activation(ctx_h[0:rows, a, :], ctx_t[p][0:rows, a, :], ACT.Copy).then_inc(s_ch, 1)
                if has_b:
                    if isinstance(s, int) and s <= FIRST_K:
                        act.wait_ge(s_raw_first, 16 * FIRST_K)
                    else:
                        act.wait_ge(s_raw_rest, 16 * (KD - FIRST_K))
                    split_high(s - 1, wh[0])
                if isinstance(s, int) and s == B:
                    early.append(load_early(act))
                    with act.If(early[0] > 0):
                        split_tile(0, 0)
                if not isinstance(s, int) or s + 1 < B:
                    if not isinstance(s, int) or s > 0:
                        normalise_queries(s + 1)
                    turned(s + 1, 0, kT[:, 0, :], KV)
                if has_a:
                    act.wait_ge(s_negmax, s + 1)
                    after(act, s_coef, s)
                    nc.scalar.activation(probs[:, :], score_ps, ACT.Exp, bias=neg_max[:, :],
                                         accum_out=prob_sum[:, :]).then_inc(s_probs, 1)

            turned(0, 0, kT[:, 0, :], KV)
            stage1(act, step)
            act.wait_ge(s_slot_token, 1)
            act.wait_ge(s_hstore, 16 * B)
            act.wait_ge(s_hnstore, 16 * B)

            def weights(e, p, ks):
                for k in ks:
                    if not (isinstance(e, int) and e == 1):
                        act.wait_ge(s_wfree, KD * (e - 2) + k + 1)
                    act.wait_ge(s_raw[k], 16 * e)
                    split_high(k, wh[p])

            def expert(e, p, last):
                over = act.value_load(tile_table[0:1, 0, bass.ds(e, 1)], min_val=0, max_val=OVER)
                over_before = act.value_load(tile_table[0:1, 1, bass.ds(e, 1)], min_val=0, max_val=OVER * E)

                def split_over(j):
                    act.wait_ge(o_xT, over_before + j + 1)
                    split_rows(xh_over).then_inc(o_xh, 1)

                if not last:
                    weights(e + 1, 1 - p, range(0, 2))
                split_tile(e, 1)
                if not last:
                    weights(e + 1, 1 - p, range(2, 5))
                with act.If(over > 0):
                    split_over(0)
                if not last:
                    weights(e + 1, 1 - p, range(5, KD))
                with act.If(over > 1):
                    with act.Fori(1, OVER) as j:
                        with act.If(over > j):
                            act.wait_ge(o_mm, over_before + j)
                            split_over(j)
                    act.nop()
                if not last:
                    split_tile(e + 1, 0)

            act.wait_ge(s_table, 1)
            with act.If(early[0] < 1):
                split_tile(0, 0)
            stage3(act, expert)

        @block.vector
        def _(dve):
            def measure(b, column):
                rows = of_batch(x_all, b)
                for half in range(2):
                    last = nc.vector.bn_stats(stats[:, column, half, :], rows[:, half * 512:(half + 1) * 512])
                return last

            def norm_link(call, made):
                def link(last, alone=False):
                    made[0] += 1
                    last.then_inc(s_norm, 1)
                    if alone:
                        wait_apart(dve, s_norm, NORM_STEPS * call + made[0])
                    else:
                        dve.wait_ge(s_norm, NORM_STEPS * call + made[0])
                return link

            def newton(link, j, cols):
                r0 = guess[j][:, cols]
                r1 = guess[j + 1][:, cols] if j + 1 < NEWTON else inv_std[:, cols]
                link(nc.vector.tensor_tensor(guess_sq[:, cols], r0, r0, ALU.mult))
                link(nc.vector.tensor_tensor(guess_sq[:, cols], guess_sq[:, cols], neg_half[:, cols], ALU.mult))
                link(nc.vector.scalar_tensor_tensor(out=r1, in0=guess_sq[:, cols], scalar=1.5, in1=r0,
                                                    op0=ALU.add, op1=ALU.mult))

            def norm_and_choose(call, measured=None, cols=None, chosen_batch=None):
                made = [0]
                link = norm_link(call, made)
                choice = chosen_batch is not None
                if measured is not None:
                    link(measured, True)
                if choice:
                    dve.wait_ge(s_logit_ps, chosen_batch + 1)
                    last = nc.vector.tensor_tensor(logit[:, :], logit_ps, bg[0:Q, :], ALU.add)
                    other = logit[:, :].unsqueeze(1).to_broadcast([Q, E, E])
                    own = logit[:, :].unsqueeze(2).to_broadcast([Q, E, E])
                if cols is not None:
                    for c in range(cols.start, cols.stop):
                        last = nc.vector.bn_aggr(mean_var[:, c, :], stats[:, c, :, :])
                link(last)
                if choice:
                    nc.vector.tensor_tensor(above[:, :, :], other, own, ALU.is_gt)
                    last = nc.vector.tensor_tensor(tied[:, :, :], other, own, ALU.is_equal)
                if cols is not None:
                    last = nc.vector.tensor_scalar(var_eps[:, cols], mean_var[:, cols, 1], EPS, None, ALU.add)
                link(last)
                if choice:
                    last = nc.vector.tensor_tensor(tied[:, :, :], tied[:, :, :], lower_e[:, :, :], ALU.mult)
                if cols is not None:
                    nc.vector.tensor_scalar(neg_half[:, cols], var_eps[:, cols], -0.5, None, ALU.mult)
                    last = nc.vector.tensor_scalar(half_bits[:, cols], var_eps[:, cols].bitcast(I32), 1, -1,
                                                   ALU.logical_shift_right, ALU.bitwise_xor)
                link(last, True)
                if cols is not None:
                    last = nc.vector.tensor_tensor(guess[0][:, cols].bitcast(I32), half_bits[:, cols],
                                                   seed_bits[:, cols], ALU.add)
                if choice:
                    last = nc.vector.tensor_tensor(above[:, :, :], above[:, :, :], tied[:, :, :], ALU.add)
                link(last)
                if choice:
                    last = nc.vector.tensor_reduce(place[:, :], above[:, :, :], AX.X, ALU.add)
                if cols is not None:
                    newton(link, 0, cols)
                else:
                    link(last)
                if choice:
                    nc.vector.tensor_scalar(chosen[:, :], place[:, :], float(TOP_K), None, ALU.is_lt).then_inc(s_chosen, 1)
                    nc.vector.tensor_tensor(onehot[:, :, :], place[:, :].unsqueeze(1).to_broadcast([Q, TOP_K, E]),
                                            choice_no[:, :, :], ALU.is_equal).then_inc(s_chosen_own, 1)
                if cols is not None:
                    for j in range(1, NEWTON - 1):
                        newton(link, j, cols)
                    assert made[0] == NORM_STEPS - 3

            def finish_norm(call, cols, ready):
                newton(norm_link(call, [NORM_STEPS - 3]), NEWTON - 1, cols)
                nc.vector.scalar_tensor_tensor(out=shift[:, cols], in0=mean_var[:, cols, 0], scalar=-1.0,
                                               in1=inv_std[:, cols], op0=ALU.mult, op1=ALU.mult).then_inc(ready, 1)

            def locate(b):
                base = SLOT_STEPS * b
                made = [0]

                def link(ins):
                    made[0] += 1
                    ins.then_inc(s_slot, 1)
                    dve.wait_ge(s_slot, base + made[0])

                dve.wait_ge(s_rank, b + 1)
                link(nc.vector.tensor_tensor(slot_of[:, :], rank_ps, expert_base[:, :], ALU.add))
                dve.wait_ge(s_chosen_own, b + 1)
                link(nc.vector.tensor_tensor(picked[:, :, :], slot_of[:, :].unsqueeze(1).to_broadcast([Q, TOP_K, E]),
                                             onehot[:, :, :], ALU.mult))
                with nc.allow_low_precision(reason="whole numbers below 2**13"):
                    link(nc.vector.tensor_reduce(slot_i[:, :], picked[:, :, :], AX.X, ALU.add))
                nc.vector.tensor_scalar(slot_col_i[:, :], slot_i[:, :], 7, None, ALU.logical_shift_right)
                link(nc.vector.tensor_scalar(slot_row_i[:, :], slot_i[:, :], P - 1, None, ALU.bitwise_and))
                nc.vector.tensor_copy(slot_col[:, :], slot_col_i[:, :])
                link(nc.vector.tensor_copy(slot_row[:, :], slot_row_i[:, :]))
                assert made[0] == SLOT_STEPS
                for c in range(TOP_K):
                    nc.vector.tensor_scalar(at_row[:, c, :], iota_slot[:, :], slot_row[:, c:c + 1], None, ALU.is_equal)
                    last = nc.vector.tensor_scalar(tok_col[:, c, :], iota_col[:, :], slot_col[:, c:c + 1],
                                                   tok_far[:, bass.ds(b, 1)], ALU.is_equal, ALU.mult)
                last.then_inc(s_tok_col, 1)
                nc.vector.tensor_tensor(chosen_sum[:, :], chosen_sum[:, :], chosen[:, :], ALU.add).then_inc(s_sum, 1)

            def add_slots(b):
                dve.wait_ge(s_slots_ps, b + 1)
                after(dve, s_acc, b)
                nc.vector.tensor_tensor(slot_acc[:, :], slot_acc[:, :], slot_ps, ALU.add).then_inc(s_acc, 1)

            def start_early():
                dve.wait_ge(s_acc, B - 2)
                nc.vector.tensor_scalar(used[:, 0:1], slot_acc[:, 0:1], 0.0, used_shift[:, 0:1], ALU.is_lt,
                                        ALU.mult).then_inc(s_early_step, 1)
                dve.wait_ge(s_early_step, 1)
                nc.vector.scalar_tensor_tensor(out=early_token[:, :], in0=slot_acc[:, 0:1], scalar=spare_row[:, 0:1],
                                               in1=used[:, 0:1], op0=ALU.add, op1=ALU.add)
                dve.wait_ge(s_early_count, 1)
                nc.vector.tensor_scalar(early_flag[:, :], count_ps[0:1, 0:1], float(P), None, ALU.is_ge
                                        ).then_inc(s_early, 1)

            def turned(s, g, dst, cols):
                dve.wait_ge(s_turned, group(s, g) + 1)
                nc.vector.tensor_copy(dst, group_bank(s, g)[:, 0:cols]).then_inc(s_evac[1], 1)

            dve.wait_ge(s_const, 1)
            dve.wait_ge(s_x0, 16)
            norm_and_choose(0, measure(0, 0), slice(0, 1))
            finish_norm(0, slice(0, 1), s_xln)

            def columns(s):
                return slice(x_late.start if isinstance(s, int) and s == 1 else B, B + 1)

            def split_rows(low, high):
                return nc.vector.tensor_tensor(low[:, :, :].rearrange("p k m -> p (k m)"), xT_ps[:, :],
                                               high[:, :, :].rearrange("p k m -> p (k m)"), ALU.subtract)

            def split_tile(e, t):
                dve.wait_ge(s_xh[t], e + 1)
                split_rows(xl[t], xh[t]).then_inc(s_xl[t], 1)

            early = []

            def step(s, p):
                has_a, has_b, has_c, has_d = parts(s)
                if has_a:
                    for g in range(1, KD - 4, 2):
                        turned(s, g, kT[:, g, :], KV)
                if isinstance(s, int) and s == 1:
                    finish_norm(1, slice(x_early.start, x_early.stop), s_xln)
                elif not isinstance(s, int) or 2 <= s <= B + 1:
                    if has_d:
                        wait_apart(dve, s_hn, s - 2)
                    finish_norm(s, columns(s - 1), s_hln)
                if has_a:
                    turned(s, KD - 3, kT[:, KD - 3, :], KV)
                if has_b:
                    dve.wait_ge(s_pTh, s)
                    rows = KV_T[LAST][1]
                    nc.vector.tensor_tensor(probsT_l[:, 0:LAST, :].rearrange("p a q -> p (a q)"), probsT_ps[:, 0:LAST * Q],
                                            probsT_h[:, 0:LAST, :].rearrange("p a q -> p (a q)"), ALU.subtract)
                    nc.vector.tensor_tensor(probsT_l[0:rows, LAST, :], probsT_ps[0:rows, LAST * Q:(LAST + 1) * Q],
                                            probsT_h[0:rows, LAST, :], ALU.subtract).then_inc(s_pTl, 1)
                if has_a:
                    turned(s, KD - 1, kT[:, KD - 1, :], KV)
                    turned(s, KD + 1, qT[:, 4:8, :].rearrange("p k q -> p (k q)"), 4 * Q)
                if has_b:
                    dve.wait_ge(s_tanh, 2)
                    dve.wait_ge(s_probs, s)
                    nc.vector.reciprocal(inv_sum[:, :], prob_sum[:, :]).then_inc(s_inv, 1)
                    dve.wait_ge(s_inv, s)
                    nc.vector.tensor_tensor(coef[:, :], inv_sum[:, :], tgx[0:Q, :], ALU.mult).then_inc(s_coef, 1)
                if isinstance(s, int) and s == 0:
                    dve.wait_ge(s_x_early, 16)
                    for b in x_early:
                        measured = measure(b, b)
                    norm_and_choose(1, measured, slice(x_early.start, x_early.stop))
                if isinstance(s, int) and s == 1:
                    dve.wait_ge(s_x_late, 16)
                    for b in x_late:
                        measure(b, b)
                if has_d:
                    locate(s - 3)
                if isinstance(s, int) and s == B:
                    add_slots(s - 3)
                    start_early()
                if has_b:
                    dve.wait_ge(s_coef, s)
                    dve.wait_ge(s_att, s)
                    rows = of_batch(x_all, s - 1)
                    nc.vector.scalar_tensor_tensor(out=rows, in0=att_ps, scalar=coef[:, 0:1], in1=rows,
                                                   op0=ALU.mult, op1=ALU.add).then_inc(s_h, 1)
                if has_c:
                    turned(s, NEW + 1, hnT[:, 4:8, :].rearrange("p k q -> p (k q)"), 4 * Q)
                if has_d and not (isinstance(s, int) and s == B):
                    add_slots(s - 3)
                if isinstance(s, int) and s == B + 1:
                    early.append(load_early(dve))
                    with dve.If(early[0] > 0):
                        split_tile(0, 0)
                if has_b:
                    wait_apart(dve, s_h, s)
                    norm_and_choose(s + 1, measure(s - 1, B), columns(s), s - 2 if has_c else None)
                elif has_c:
                    norm_and_choose(s + 1, chosen_batch=s - 2)
                if has_a:
                    dve.wait_ge(s_scores, s + 1)
                    after(dve, s_probs, s)
                    nc.vector.tensor_reduce(neg_max[:, :], score_ps, AX.X, ALU.max, negate=True).then_inc(s_negmax, 1)

            def split_low(e, k, p):
                dve.wait_ge(s_wh, KD * (e + 1) + k + 1)
                nc.vector.tensor_tensor(at_k(wl[p], k), at_k(raw, k), at_k(wh[p], k), ALU.subtract).then_inc(s_wl, 1)

            stage1(dve, step)

            made = [0]

            def link(ins):
                made[0] += 1
                ins.then_inc(s_last, 1)
                dve.wait_ge(s_last, made[0])

            dve.wait_ge(s_acc, B)
            link(nc.vector.tensor_scalar(used[:, :], slot_acc[:, :], 0.0, used_shift[:, 0:1], ALU.is_lt, ALU.mult))
            nc.vector.scalar_tensor_tensor(out=slot_token[:, :], in0=slot_acc[:, :], scalar=spare_row[:, 0:1],
                                           in1=used[:, :], op0=ALU.add, op1=ALU.add).then_inc(s_slot_token, 1)
            dve.wait_ge(s_count, 1)
            link(nc.vector.tensor_scalar(over_f[:, :], count_ps[0:1, :], float(-STATIC_TILES * P + P - 1), 0.0,
                                         ALU.add, ALU.max))
            link(nc.vector.tensor_copy(over_i[:, :], over_f[:, :]))
            link(nc.vector.tensor_scalar(tile_table[:, 0, :], over_i[:, :], 7, None, ALU.logical_shift_right))
            link(nc.vector.tensor_copy(over_e[:, :], tile_table[:, 0, :]))
            link(nc.vector.tensor_tensor(over_m[:, :, :], lower_e[0:1, :, :],
                                         over_e[:, :].unsqueeze(1).to_broadcast([1, E, E]), ALU.mult))
            link(nc.vector.tensor_reduce(over_b[:, :], over_m[:, :, :], AX.X, ALU.add))
            nc.vector.tensor_copy(tile_table[:, 1, :], over_b[:, :]).then_inc(s_table, 1)
            dve.wait_ge(s_hstore, 16 * B)
            dve.wait_ge(s_hnstore, 16 * B)

            dve.wait_ge(s_tgf, 1)
            dve.nop().then_inc(o_yev, 1)

            def weights(e, p, ks):
                for k in ks:
                    split_low(e - 1, k, p)

            def finish(banks, dst, evacuated_sem, n, ready):
                nc.vector.tensor_tensor(dst[:, :], banks[:, :], bias[:, :], ALU.add).then_inc(evacuated_sem, 1)
                dve.wait_ge(evacuated_sem, n)
                nc.vector.tensor_scalar(dst[:, :], dst[:, :], 0.0, tgf_half[:, 0:1], ALU.max, ALU.mult
                                        ).then_inc(ready, 1)

            def evacuate(e, t):
                if t == 0:
                    dve.wait_ge(s_mm0, e + 1)
                else:
                    dve.wait_ge(s_wfree, KD * e + KD)
                dve.wait_ge(s_bias, 16 * e + 16)
                if not (isinstance(e, int) and e == 0 and t == 0):
                    dve.wait_ge(s_added, 16 * (2 * e + t))
                finish(y_ps[t], y, s_yev[t], e + 1, s_y)

            def expert(e, p, last):
                over = dve.value_load(tile_table[0:1, 0, bass.ds(e, 1)], min_val=0, max_val=OVER)
                over_before = dve.value_load(tile_table[0:1, 1, bass.ds(e, 1)], min_val=0, max_val=OVER * E)

                def split_over(j):
                    dve.wait_ge(o_xh, over_before + j + 1)
                    split_rows(xl_over, xh_over).then_inc(o_xl, 1)

                def evacuate_over(j):
                    n = over_before + j
                    dve.wait_ge(o_mm, n + 1)
                    finish(over_ps, over_rows, o_yev, n + 2, o_y)

                if not last:
                    weights(e + 1, 1 - p, range(0, 2))
                split_tile(e, 1)
                if not last:
                    weights(e + 1, 1 - p, range(2, 5))
                with dve.If(over > 0):
                    split_over(0)
                evacuate(e, 0)
                if not last:
                    weights(e + 1, 1 - p, range(5, KD))
                with dve.If(over > 0):
                    evacuate_over(0)
                    with dve.If(over > 1):
                        with dve.Fori(1, OVER) as j:
                            with dve.If(over > j):
                                split_over(j)
                                evacuate_over(j)
                        dve.nop()
                    dve.nop()
                if not last:
                    split_tile(e + 1, 0)
                evacuate(e, 1)

            dve.wait_ge(s_table, 1)
            with dve.If(early[0] < 1):
                split_tile(0, 0)
            stage3(dve, expert)

        @block.gpsimd
        def _(pool):
            made = [0]

            def link(ins):
                made[0] += 1
                ins.then_inc(s_const0, 1)
                return made[0]

            g = nc.gpsimd
            link(g.memset(ident[:, :], 0.0))
            link(g.memset(before[:, :], 1.0))
            link(g.memset(lower_e[:, :, :], 1.0))
            link(g.memset(raw[:, KD - 1, :], 0.0))
            link(g.iota(seed_bits[:, :], [[0, B + 1]], base=SEED_BITS, channel_multiplier=0))
            link(g.memset(ones[:, :], 1.0))
            link(g.memset(chosen_sum[:, :], 0.0))
            link(g.memset(slot_acc[:, :], 0.0))
            link(g.iota(choice_no[:, :, :], [[1, TOP_K], [0, E]], base=0, channel_multiplier=0,
                        allow_small_or_imprecise_dtypes=True))
            link(g.iota(iota_slot[:, :], [[1, P]], base=0, channel_multiplier=0, allow_small_or_imprecise_dtypes=True))
            link(g.iota(iota_col[:, :], [[1, COLS]], base=0, channel_multiplier=0, allow_small_or_imprecise_dtypes=True))
            link(g.iota(expert_base[:, :], [[MAX_TILES * P, E]], base=0, channel_multiplier=0,
                        allow_small_or_imprecise_dtypes=True))
            link(g.iota(tok_far[:, :], [[Q, B]], base=-FAR, channel_multiplier=1, allow_small_or_imprecise_dtypes=True))
            link(g.iota(spare_row[:, :], [[0, 1]], base=N_TOK, channel_multiplier=1, allow_small_or_imprecise_dtypes=True))
            link(g.iota(used_shift[:, :], [[0, 1]], base=FAR - N_TOK, channel_multiplier=-1,
                        allow_small_or_imprecise_dtypes=True))
            pool.wait_ge(s_const0, made[0])
            link(g.affine_select(out=ident[:, :], in_=ident[:, :], compare_op=ALU.not_equal, fill=1.0, base=0,
                                 pattern=[[-1, P]], channel_multiplier=1))
            link(g.affine_select(out=before[:, :], in_=before[:, :], compare_op=ALU.is_gt, fill=0.0, base=0,
                                 pattern=[[1, Q]], channel_multiplier=-1))
            link(g.affine_select(out=lower_e[:, :, :], in_=lower_e[:, :, :], compare_op=ALU.is_gt, fill=0.0, base=0,
                                 pattern=[[1, E], [-1, E]], channel_multiplier=0))
            pool.wait_ge(s_const0, made[0])
            pool.nop().then_inc(s_const, 1)
            for rows in (out, hn_rows):
                g.dma_start(rows[N_TOK:N_TOK + P, :], raw[:, KD - 1, :]).then_inc(s_zero, 16)

            def gather(dst, idx, done_sem, rows=hn_rows):
                g.indirect_dma_start(dst[:, :], None, rows, bass.IndirectOffsetOnAxis(idx, 0)).then_inc(done_sem, 16)

            def gather_tile(e, t, p, tokens=None, rows=hn_rows):
                idx = idx_now[:, 2 * p + t:2 * p + t + 1]
                if not (isinstance(e, int) and e == 0):
                    pool.wait_ge(s_xT[t], e)
                if not (isinstance(e, int) and e < 2):
                    pool.wait_ge(s_added, 32 * (e - 2) + 16 * t + 16)
                if tokens is None:
                    tokens = slot_token[:, bass.ds(e * MAX_TILES + t, 1)]
                g.tensor_copy(idx, tokens).then_inc(s_idx, 1)
                wait_apart(pool, s_idx, 2 * e + t + 1)
                gather(xg[t], idx, s_gath[t], rows)

            early = []

            def step(s, p):
                has_a, has_b, has_c, _ = parts(s)
                if isinstance(s, int) and s == B:
                    early.append(load_early(pool))
                    with pool.If(early[0] > 0):
                        pool.wait_ge(s_zero, 32)
                        pool.wait_ge(s_hnstore, 16 * (B - 2))
                        gather_tile(0, 0, 0, early_token[:, :], hn_rows[0:(B - 2) * Q, :])
                if has_c:
                    wait_apart(pool, s_hn, s - 1)
                    g.dma_start(hn_rows[bass.ds((s - 2) * Q, Q), :], normed[:, :]).then_inc(s_hnstore, 16)
                if has_b:
                    wait_apart(pool, s_h, s)
                    g.dma_start(out[bass.ds((s - 1) * Q, Q), :], of_batch(x_all, s - 1)).then_inc(s_hstore, 16)
                if has_a:
                    for a, (_, rows) in enumerate(KV_T):
                        pool.wait_ge(s_ch, 3 * s + a + 1)
                        last = g.tensor_tensor(ctx_l[0:rows, a, :], ctx_t[p][0:rows, a, :], ctx_h[0:rows, a, :],
                                               ALU.subtract)
                    last.then_inc(s_cl, 1)
                if has_b:
                    pool.wait_ge(s_wh, s)
                    g.tensor_tensor(at_k(wl[0], s - 1), at_k(raw, s - 1), at_k(wh[0], s - 1),
                                    ALU.subtract).then_inc(s_wl0, 1)

            stage1(pool, step)

            pool.wait_ge(s_slot_token, 1)
            pool.wait_ge(s_zero, 32)
            pool.wait_ge(s_hstore, 16 * B)
            pool.wait_ge(s_hnstore, 16 * B)

            def add_rows(rows, idx, added):
                g.indirect_dma_start(out, bass.IndirectOffsetOnAxis(idx, 0), rows[:, :], None,
                                     compute_op=ALU.add).then_inc(added, 16)

            def add_tile(e, t, p):
                pool.wait_ge(s_y, 2 * e + t + 1)
                if not (isinstance(e, int) and e == 0 and t == 0):
                    wait_apart(pool, s_added, 16 * (2 * e + t))
                add_rows(y, idx_now[:, 2 * p + t:2 * p + t + 1], s_added)

            def table(e):
                return (pool.value_load(tile_table[0:1, 0, bass.ds(e, 1)], min_val=0, max_val=OVER),
                        pool.value_load(tile_table[0:1, 1, bass.ds(e, 1)], min_val=0, max_val=OVER * E))

            idx_over = idx_now[:, 2 * STATIC_TILES:2 * STATIC_TILES + 1]

            def gather_over(e, over_before, j):
                tokens = slot_token[:, bass.ds(e * MAX_TILES + STATIC_TILES + j, 1)]
                g.tensor_copy(idx_over, tokens).then_inc(o_idx, 1)
                wait_apart(pool, o_idx, over_before + j + 1)
                gather(over_rows, idx_over, o_gath)

            def gather_first_over(e):
                over, over_before = table(e)
                with pool.If(over > 0):
                    gather_over(e, over_before, 0)

            def expert(e, p, last):
                over, over_before = table(e)

                def add_over(j):
                    n = over_before + j
                    wait_apart(pool, o_y, n + 1)
                    add_rows(over_rows, idx_over, o_added)
                    wait_apart(pool, o_added, 16 * n + 16)

                if not last:
                    gather_tile(e + 1, 0, 1 - p)
                    gather_tile(e + 1, 1, 1 - p)
                add_tile(e, 0, p)
                with pool.If(over > 0):
                    wait_apart(pool, s_added, 32 * e + 16)
                    add_over(0)
                    with pool.If(over > 1):
                        with pool.Fori(1, OVER) as j:
                            with pool.If(over > j):
                                gather_over(e, over_before, j)
                                add_over(j)
                        pool.nop()
                    pool.nop()
                if not last:
                    gather_first_over(e + 1)
                add_tile(e, 1, p)

            with pool.If(early[0] < 1):
                gather_tile(0, 0, 0)
            gather_tile(0, 1, 0)
            pool.wait_ge(s_table, 1)
            gather_first_over(0)
            stage3(pool, expert)
            pool.wait_ge(s_added, 16 * 2 * E)


NEWTON = 3
SEED_BITS = 0x5F3759DF + 1
NORM_STEPS = 5 + 3 * NEWTON

SLOT_STEPS = 5

_INS = ["x", "ctx_4096", "g_xattn", "g_ffn", "L0_ffn_W_gate", "L0_ffn_b_gate", "L0_ffn_W_e", "L0_ffn_b_e"]


def kernel(**inputs):
    import numpy as np
    import concourse.bacc as bacc
    from concourse.bass_utils import run_bass_kernel_spmd

    nc = bacc.Bacc("TRN2", target_bir_lowering=False, num_devices=1)
    arrays, args = {}, []
    for name in _INS:
        a = np.ascontiguousarray(inputs[name])
        arrays[f"in_{name}"] = a
        args.append(nc.dram_tensor(f"in_{name}", a.shape, mybir.dt.from_np(a.dtype), kind="ExternalInput").ap())
    b, q, d = inputs["x"].shape
    out = nc.dram_tensor("out_rows", [b * q + P, d], F32, kind="ExternalOutput").ap()
    gated_block(nc, *args, out)
    r = run_bass_kernel_spmd(nc, [arrays], core_ids=[0])
    return r.results[0]["out_rows"][:b * q].reshape(b, q, d)
```
